# Optimizing a Trainium2 kernel written in Bass

```python
import numpy as np
import jax
import jax.numpy as jnp

def _softmax(x, axis=-1):
    return jax.nn.softmax(x, axis=axis)

def _gelu(x):
    return jax.nn.gelu(x, approximate=True)

def _silu(x):
    return jax.nn.silu(x)

def _sigmoid(x):
    return jax.nn.sigmoid(x)

def _layernorm(x, axis=-1, eps=1e-05):
    m = jnp.mean(x, axis=axis, keepdims=True)
    v = jnp.var(x, axis=axis, keepdims=True)
    return (x - m) / jnp.sqrt(v + eps)

def _scatter_add(tgt, idx, src, axis=0):
    return tgt.at[idx].add(src)

def _segment_sum(src, seg, n):
    return jax.ops.segment_sum(src, seg, n)
kernel_name = 'mk_flamingo_gated_d1_seqx_r2_3d3e7c'

def setup_inputs(seed: int=0):
    np.random.seed(seed)
    _w = jnp.asarray

    def _rec_inputs():
        import jax
        import jax.numpy as jnp
        _rk = jax.random.key(seed)
        x = -0.0003929 + 0.9999 * jax.random.normal(jax.random.fold_in(_rk, 1), (8, 224, 1024), jnp.float32)
        _lenS = 224 - jax.random.randint(jax.random.fold_in(_rk, 7), (8,), 0, max(1, 224 // 4) + 1, jnp.int32)
        _lenS2 = 750 - jax.random.randint(jax.random.fold_in(_rk, 8), (8,), 0, max(1, 750 // 4) + 1, jnp.int32)
        _ctx_2048P = jax.random.normal(jax.random.fold_in(_rk, 11), (8, 16, 1024), jnp.float32)
        _ctx_2048c = jax.random.dirichlet(jax.random.fold_in(_rk, 511), 0.3 * jnp.ones((16,), jnp.float32), (8, 750))
        _ctx_2048t = jnp.einsum('bsk,bkd->bsd', _ctx_2048c, _ctx_2048P)
        _ctx_2048t = _ctx_2048t * jax.lax.rsqrt(jnp.mean(jnp.square(_ctx_2048t)) + 1e-12) * 0.953939
        ctx_2048 = -0.000514642 + 1.00011 * (_ctx_2048t + 0.3 * jax.random.normal(jax.random.fold_in(_rk, 611), (8, 750, 1024), jnp.float32))
        _g = jax.random.normal(jax.random.fold_in(_rk, 9001), (2, 1), jnp.float32)
        _g = jnp.sign(_g) * jnp.maximum(jnp.abs(_g), 1.0) + (_g == 0) * 1.0
        g_xattn = _g[0]
        g_ffn = _g[1]
        return (x, ctx_2048, g_xattn, g_ffn)
    x, ctx_2048, g_xattn, g_ffn = _rec_inputs()

    def _L0_xattn_setup():
        import jax, jax.numpy as jnp
        import numpy as np
        DIM = 1024
        NHEADS = 32
        HEAD_DIM = DIM // NHEADS
        EPS = 1e-06

        def _rmsnorm(t):
            return t * jax.lax.rsqrt(jnp.mean(t * t, axis=-1, keepdims=True) + EPS)
        key = jax.random.key(seed)
        kx, kc, kq, kk, kv = jax.random.split(key, 5)
        x = jax.random.normal(kx, (2, 2048, DIM), dtype=jnp.float32)
        context = jax.random.normal(kc, (2, 256, DIM), dtype=jnp.float32)
        std = 0.02
        Wq = jax.random.normal(kq, (DIM, DIM), dtype=jnp.float32) * std
        Wk = jax.random.normal(kk, (DIM, DIM), dtype=jnp.float32) * std
        Wv = jax.random.normal(kv, (DIM, DIM), dtype=jnp.float32) * std
        return {'x': x, 'context': context, 'Wq': Wq, 'Wk': Wk, 'Wv': Wv}
    _L0_xattn_all = _L0_xattn_setup()
    _L0_xattn_in = {k: v for k, v in _L0_xattn_all.items() if k in ('Wq', 'Wk', 'Wv')}
    del _L0_xattn_all

    def _L0_ffn_setup():
        import jax, jax.numpy as jnp
        import numpy as np
        EPS = 1e-08

        def _quantize(w):
            gamma = jnp.mean(jnp.abs(w))
            return jnp.clip(jnp.round(w / (gamma + EPS)), -1.0, 1.0)

        def _bitlinear(x, w):
            return jnp.matmul(x, _quantize(w).T)
        key = jax.random.key(seed)
        k1, k2, k3, k4 = jax.random.split(key, 4)
        d, h = (1024, 2816)
        x = jax.random.normal(k1, (4, 1024, d), dtype=jnp.float32)
        w1 = jax.random.normal(k2, (h, d), dtype=jnp.float32)
        w2 = jax.random.normal(k3, (h, d), dtype=jnp.float32)
        w3 = jax.random.normal(k4, (d, h), dtype=jnp.float32)
        return {'x': x, 'w1': w1, 'w2': w2, 'w3': w3}
    _L0_ffn_all = _L0_ffn_setup()
    _L0_ffn_in = {k: v for k, v in _L0_ffn_all.items() if k in ('w1', 'w2', 'w3')}
    del _L0_ffn_all
    return {'x': x, 'ctx_2048': ctx_2048, 'g_xattn': g_xattn, 'g_ffn': g_ffn, 'L0_xattn_Wq': _L0_xattn_in['Wq'], 'L0_xattn_Wk': _L0_xattn_in['Wk'], 'L0_xattn_Wv': _L0_xattn_in['Wv'], 'L0_ffn_w1': _L0_ffn_in['w1'], 'L0_ffn_w2': _L0_ffn_in['w2'], 'L0_ffn_w3': _L0_ffn_in['w3']}

def reference(x, ctx_2048, g_xattn, g_ffn, L0_xattn_Wq, L0_xattn_Wk, L0_xattn_Wv, L0_ffn_w1, L0_ffn_w2, L0_ffn_w3):
    import jax
    import jax.numpy as jnp

    def _L0_xattn_ref(x, context, Wq, Wk, Wv):
        import jax, jax.numpy as jnp
        import numpy as np
        DIM = 1024
        NHEADS = 32
        HEAD_DIM = DIM // NHEADS
        EPS = 1e-06

        def _rmsnorm(t):
            return t * jax.lax.rsqrt(jnp.mean(t * t, axis=-1, keepdims=True) + EPS)
        b, n, _ = x.shape
        m = context.shape[1]
        q = x @ Wq.T
        k_raw = context @ Wk.T
        v_raw = context @ Wv.T
        q = q.reshape(b, n, NHEADS, HEAD_DIM).transpose(0, 2, 1, 3)
        kv = jnp.concatenate([k_raw, v_raw], axis=-1)
        kv = kv.reshape(b, m, NHEADS, HEAD_DIM, 2)
        k = kv[..., 0].transpose(0, 2, 1, 3)
        v = kv[..., 1].transpose(0, 2, 1, 3)
        q = _rmsnorm(q)
        k = _rmsnorm(k)
        scale = HEAD_DIM ** (-0.5)
        scores = jnp.einsum('bhnd,bhmd->bhnm', q, k) * scale
        attn = jax.nn.softmax(scores, axis=-1)
        out = jnp.einsum('bhnm,bhmd->bhnd', attn, v)
        return out.transpose(0, 2, 1, 3).reshape(b, n, NHEADS * HEAD_DIM)

    def _L0_ffn_ref(x, w1, w2, w3):
        import jax, jax.numpy as jnp
        import numpy as np
        EPS = 1e-08

        def _quantize(w):
            gamma = jnp.mean(jnp.abs(w))
            return jnp.clip(jnp.round(w / (gamma + EPS)), -1.0, 1.0)

        def _bitlinear(x, w):
            return jnp.matmul(x, _quantize(w).T)
        x1 = _bitlinear(x, w1)
        x2 = _bitlinear(x, w2)
        hidden = jax.nn.sigmoid(x1) * x2
        return _bitlinear(hidden, w3)
    x = x + jnp.tanh(g_xattn[0]) * _L0_xattn_ref(_layernorm(x, axis=-1), ctx_2048, L0_xattn_Wq, L0_xattn_Wk, L0_xattn_Wv)
    x = x + jnp.tanh(g_ffn[0]) * _L0_ffn_ref(_layernorm(x, axis=-1), L0_ffn_w1, L0_ffn_w2, L0_ffn_w3)
    return x

_drawn_inputs = setup_inputs


def setup_inputs(seed=0):
    import zlib

    import numpy as np

    out = dict(_drawn_inputs(seed))
    spreads = {}
    factors = {}
    for name, (base, spread) in spreads.items():
        noise = np.random.default_rng([zlib.crc32(name.encode()), seed]).standard_normal(out[name].shape)
        drawn = base * np.exp(spread * noise) if base else spread * noise
        out[name] = jnp.asarray(drawn.astype(out[name].dtype))
    for name, factor in factors.items():
        out[name] = (out[name] * factor).astype(out[name].dtype)
    return out
```

```python
from contextlib import ExitStack

import concourse.bass as bass
from concourse import mybir

ALU = mybir.AluOpType
ACT = mybir.ActivationFunctionType
AX_X = mybir.AxisListType.X
F32 = mybir.dt.float32
F32R = mybir.dt.float32r
F16 = mybir.dt.float16
BF16 = mybir.dt.bfloat16

P = 128
B, S, D = 8, 224, 1024
SK = 750
NH, DH = 32, 32
F = 2816
KC = D // P
TOK = B * S
NT = TOK // P
KT, KW = 6, 125
G, HG = 4, 8
GC = HG * DH
U = G * B
NQ = 4 * KT
VW = 3 * DH + 1
SHIFT = 5
LAG = 3
QROWS = (P, S - P)
LT = 112
NL = TOK // LT
FJ = F // P
CH = ((0, 512), (512, 512), (1024, 512), (1536, 256))
MP = 2 * P
NM = TOK // MP
WPAIRS = 3 * FJ // 2
LN_EPS, RMS_EPS, Q_EPS = 1e-5, 1e-6, 1e-8
SCALE = float(DH) ** -0.5
ROOT = float(DH) ** 0.5
LN128 = 4.852030263919617


def wait(eng, sem, n):
    if not isinstance(n, int) or n > 0:
        eng.wait_ge(sem, n)


def flamingo_kernel(nc, x_d, ctx_d, wq_d, wkv_d, wffn_d, gates_d, out_d):
    qst_d = nc.dram_tensor("q_stacks", [G, P, HG, TOK], F16, kind="Internal").ap()
    att_d = nc.dram_tensor("attention", [U, S, GC], F32, kind="Internal").ap()
    x1_d = nc.dram_tensor("x_after_attention", [TOK, D], F32, kind="Internal").ap()
    hid_d = nc.dram_tensor("hidden", [P, FJ, 2, TOK], F16, kind="Internal").ap()

    top = ExitStack()

    def sem(name):
        return top.enter_context(nc.semaphore(name))

    def sb(scope, name, shape, dt):
        return scope.enter_context(nc.sbuf_tensor(name, shape, dt))

    with top:
        ident = sb(top, "ident", [P, P], F32)
        identh = sb(top, "identh", [P, P], F16)
        ones = sb(top, "ones", [P, P], F32)
        mhalf = sb(top, "mhalf", [P, 16], F32)
        mone = sb(top, "mone", [P, HG], F32)
        lneps = sb(top, "lneps", [P, 1], F32)
        rmseps = sb(top, "rmseps", [P, 16], F32)
        gates = sb(top, "gates", [P, 2], F32)
        tanhs = sb(top, "tanhs", [P, 2], F32)
        gsum = sb(top, "gsum", [P, 2 * WPAIRS], F32)
        gmat = sb(top, "gmat", [P, 3], F32)
        thr = sb(top, "thr", [P, 3, 3], F32)
        ps = top.enter_context(nc.psum_tensor("ps", [P, 8, 512], F32))

        def bank(b, dt=F32):
            v = ps[:, b, :]
            return v if dt == F32 else v.bitcast(dt)

        ab = ExitStack()
        wkraw = sb(ab, "wkraw", [P, KC, 512], F32)
        wkhi = sb(ab, "wkhi", [P, KC, 512], F32R)
        wklo = sb(ab, "wklo", [P, KC, 512], F32R)

        pa = ExitStack()
        wqraw = sb(pa, "wqraw", [P, 4, D], F32)
        wqhi = sb(pa, "wqhi", [P, KC, D], F32R)
        wqlo = sb(pa, "wqlo", [P, KC, D], F32R)
        xraw = sb(pa, "xraw", [P, 2, D], F32)
        xn = sb(pa, "xn", [P, D], F32)
        xhi = sb(pa, "xhi", [P, 2, D], F32R)
        xlo = sb(pa, "xlo", [P, 2, D], F32R)
        qsq = sb(pa, "qsq", [P, 16, DH], F32)
        qhat = sb(pa, "qhat", [P, 16, DH], F32)
        qnat = sb(pa, "qnat", [P, 2, 16, 4, DH], F16)
        qTs = sb(pa, "qTs", [P, 2, 16, P], F16)
        bst = sb(pa, "bst", [P, 2, 6], F32)
        bag = sb(pa, "bag", [P, 2, 2], F32)
        vep = sb(pa, "vep", [P, 1], F32)
        xrs = sb(pa, "xrs", [P, 2, 1], F32)
        qss = sb(pa, "qss", [P, 16], F32)
        qms = sb(pa, "qms", [P, 16], F32)
        qrs = sb(pa, "qrs", [P, 16], F32)
        pa.close()

        pb = ExitStack()
        craw = sb(pb, "craw", [P, 3, KC, KW], F32)
        chi = sb(pb, "chi", [P, 2, KC, KW], F32R)
        clo = sb(pb, "clo", [P, 2, KC, KW], F32R)
        kst = sb(pb, "kst", [P, 2, HG, SK], F16)
        val = sb(pb, "val", [P, 2, KT, HG, VW], BF16)
        qT = sb(pb, "qT", [P, 2, HG, S], F16)
        pf = sb(pb, "pf", [P, 6, 2 * S], F32)
        phi = sb(pb, "phi", [P, 6, 2, S], F16)
        plo = sb(pb, "plo", [P, 6, 2, S], F16)
        ksq = sb(pb, "ksq", [P, HG, DH], F32)
        khat = sb(pb, "khat", [P, HG, DH], F32)
        knat = sb(pb, "knat", [P, 2, HG, 4, DH], F16)
        vres = sb(pb, "vres", [P, HG, DH], F32)
        kss = sb(pb, "kss", [P, HG], F32)
        kms = sb(pb, "kms", [P, HG], F32)
        krs = sb(pb, "krs", [P, HG], F32)
        oraw = sb(pb, "oraw", [P, 2, 2, HG, VW], F32)
        osum = sb(pb, "osum", [P, HG, DH], F32)
        oinv = sb(pb, "oinv", [P, HG], F32)
        oatt = sb(pb, "oatt", [P, 2, 2, HG, DH], F32)
        gbuf = sb(pb, "gbuf", [P, 2, 2, D], F32)
        pb.close()
        ab.close()

        w3q = sb(top, "w3q", [P, FJ, D], BF16)
        pc = ExitStack()
        xnTh = sb(pc, "xnTh", [P, KC, TOK], F16)
        xnTl = sb(pc, "xnTl", [P, KC, TOK], F16)
        cx = sb(pc, "cx", [LT, 2, D], F32)
        ca = sb(pc, "ca", [LT, 2, D], F32)
        cn = sb(pc, "cn", [LT, 2, D], F32)
        cnh = sb(pc, "cnh", [LT, 2, D], F16)
        cnl = sb(pc, "cnl", [LT, 2, D], F16)
        cst = sb(pc, "cst", [LT, 2, 6], F32)
        cag = sb(pc, "cag", [LT, 2, 2], F32)
        cve = sb(pc, "cve", [LT, 1], F32)
        crs = sb(pc, "crs", [LT, 2, 1], F32)
        wraw = sb(pc, "wraw", [P, 2, 3, D], F32)
        wneg = sb(pc, "wneg", [P, D], BF16)
        w12q = sb(pc, "w12q", [P, 2, 2, KC, P], BF16)
        sg = sb(pc, "sg", [P, 2, 512], F32)
        hf = sb(pc, "hf", [P, 2, 512], F32)
        hh = sb(pc, "hh", [P, 2, 2, 512], F16)
        pc.close()
        pd = ExitStack()
        hid = sb(pd, "hid", [P, 2, FJ, 2, MP], F16)
        x1b = sb(pd, "x1b", [P, 2, D], F32)
        ob = sb(pd, "ob", [P, 2, D], F32)
        pd.close()

        consts_ready = sem("consts_ready")
        gates_in = sem("gates_in"); tanh_ready = sem("tanh_ready")
        wq_in = [sem(f"wq_in{i}") for i in range(4)]
        wqhi_ready = sem("wqhi_ready"); wqlo_ready = sem("wqlo_ready")
        x_in = [sem(f"x_in{i}") for i in range(2)]
        mv_ready = sem("mv_ready"); vep_ready = sem("vep_ready")
        xrs_ready = sem("xrs_ready"); xn_ready = sem("xn_ready"); xT_ready = sem("xT_ready")
        xhi_ready = sem("xhi_ready"); xlo_ready = sem("xlo_ready")
        q_ready = sem("q_ready"); qsq_ready = sem("qsq_ready"); qss_ready = sem("qss_ready")
        qms_ready = sem("qms_ready"); qrs_ready = sem("qrs_ready"); qhat_ready = sem("qhat_ready")
        qhi_ready = sem("qhi_ready"); qlo_ready = sem("qlo_ready"); qT_ready = sem("qT_ready")
        qTa_ready = sem("qTa_ready"); qTb_ready = sem("qTb_ready")
        q_saved = [sem(f"q_saved{i}") for i in range(2)]

        wk_in = sem("wk_in"); wkhi_ready = sem("wkhi_ready"); wklo_ready = sem("wklo_ready")
        ctx_in = [sem(f"ctx_in{i}") for i in range(3)]
        q_in = [sem(f"q_in{i}") for i in range(2)]
        gw_in = [sem(f"gw_in{i}") for i in range(2)]
        chi_ready = sem("chi_ready"); clo_ready = sem("clo_ready"); kv_ready = sem("kv_ready")
        ksq_ready = sem("ksq_ready"); kss_ready = sem("kss_ready"); kms_ready = sem("kms_ready")
        krs_ready = sem("krs_ready"); khat_ready = sem("khat_ready"); khi_ready = sem("khi_ready")
        klo_ready = sem("klo_ready"); kT_ready = sem("kT_ready"); kst_ready = sem("kst_ready")
        v1_ready = sem("v1_ready"); vres_ready = sem("vres_ready"); v2_ready = sem("v2_ready")
        v3_ready = sem("v3_ready")
        s_ready = sem("s_ready"); p_ready = sem("p_ready"); phi_ready = sem("phi_ready")
        plo_ready = sem("plo_ready"); pv_done = sem("pv_done"); o_ready = sem("o_ready")
        pool_step = sem("pool_step"); att_ready = sem("att_ready")
        att_saved = [sem(f"att_saved{i}") for i in range(2)]
        gsum_ready = sem("gsum_ready"); gmat_ready = sem("gmat_ready")
        gall_ready = sem("gall_ready"); thr_step = sem("thr_step")

        lx_in = [sem(f"lx_in{i}") for i in range(2)]
        x1_ready = sem("x1_ready"); x1_saved = [sem(f"x1_saved{i}") for i in range(2)]
        lmv_ready = sem("lmv_ready"); lve_ready = sem("lve_ready")
        lrs_ready = sem("lrs_ready"); cn_ready = sem("cn_ready"); cnh_ready = sem("cnh_ready")
        cnl_ready = sem("cnl_ready"); cnT_ready = sem("cnT_ready")
        xnTh_ready = sem("xnTh_ready"); xnTl_ready = sem("xnTl_ready")
        w_in = [sem(f"w_in{i}") for i in range(2)]
        wneg_ready = sem("wneg_ready"); wquant_ready = sem("wquant_ready")
        h_ready = sem("h_ready"); sg_ready = sem("sg_ready"); hf_ready = sem("hf_ready")
        hh_ready = sem("hh_ready"); hl_ready = sem("hl_ready")
        hid_saved = [sem(f"hid_saved{i}") for i in range(2)]
        hid_in = [sem(f"hid_in{i}") for i in range(2)]
        x1_in = [sem(f"x1_in{i}") for i in range(2)]
        y_ready = sem("y_ready"); ob_ready = sem("ob_ready")
        out_saved = [sem(f"out_saved{i}") for i in range(2)]

        def tiles_of_x(eng, step):
            for i in range(2):
                step(i, i, False)
            with eng.Fori(1, NT // 2 - 1) as pair:
                for s in range(2):
                    step(pair * 2 + s, s, False)
            for i in (NT - 2, NT - 1):
                step(i, i % 2, i)

        def units(eng, unit, group=None):
            if group:
                group(0)
            for u in range(4):
                unit(u, u % 2, min(u, 2), u, 0)
            with eng.Fori(2, B // 2) as pair:
                for s in range(2):
                    unit(pair * 2 + s, s, 2, pair * 2 + s, 0)
            with eng.Fori(1, G) as g:
                if group:
                    group(g)
                with eng.Fori(0, B // 2) as pair:
                    for s in range(2):
                        unit(g * B + pair * 2 + s, s, 2, pair * 2 + s, g)
            unit(U, 0, U, None, None)
            unit(U + 1, 1, U + 1, None, None)

        def projects(k):
            return k < U

        def attends(k, r, lag):
            return (k >= 2 or (k == 1 and r >= lag)) and k <= U or (k == U + 1 and r < lag)

        def behind(k, t, n):
            if k == 0:
                return t >= n
            return k < U or (k == U and t < n)

        def phase_a_over(eng):
            eng.wait_ge(qTa_ready, 2 * NT)
            eng.wait_ge(qTb_ready, 2 * NT)
            for c in range(2):
                eng.wait_ge(q_saved[c], 32 * NT)

        def phase_b_over(eng):
            for s in range(2):
                eng.wait_ge(att_saved[s], 32 * (U // 2))
            eng.wait_ge(gall_ready, 1)

        block = top.enter_context(nc.Block())

        @block.sync
        def _(sp):
            sp.dma_start(gates[:, :], gates_d).then_inc(gates_in, 16)
            for i in range(2):
                sp.dma_start(xraw[:, i, :], x_d[i, :, :]).then_inc(x_in[i], 16)
            for kc in range(KC):
                if kc >= 4:
                    sp.wait_ge(wqlo_ready, kc - 3)
                sp.dma_start(wqraw[:, kc % 4, :], wq_d[:, kc, :]).then_inc(wq_in[kc % 4], 16)
            sp.dma_start(wkraw[:, :, :], wkv_d[0, :, :, :]).then_inc(wk_in, 16)

            def save_q(h, i, c):
                sp.wait_ge(qTa_ready, h + 1)
                sp.wait_ge(qTb_ready, h + 1)
                for g in range(2):
                    sp.dma_start(qst_d[2 * c + g, :, :, bass.ds(i * P, P)],
                                 qTs[:, c, HG * g:HG * g + HG, :]).then_inc(q_saved[c], 16)

            def step_a(i, par, last):
                if not last:
                    sp.wait_ge(xn_ready, i + 1)
                    sp.dma_start(xraw[:, par, :], x_d[i + 2, :, :]).then_inc(x_in[par], 16)
                if not (isinstance(i, int) and i == 0):
                    save_q(2 * i - 2, i - 1, 0)
                    save_q(2 * i - 1, i - 1, 1)

            tiles_of_x(sp, step_a)
            for c in range(2):
                save_q(2 * NT - 2 + c, NT - 1, c)
                sp.wait_ge(q_saved[c], 32 * NT)

            def load_ctx(T, slot, idx):
                wait(sp, clo_ready, T - 2)
                sp.dma_start(craw[:, slot, :, :], ctx_d[idx, :, :, :]).then_inc(ctx_in[slot], 16)

            def save_att(a, par):
                sp.wait_ge(att_ready, 2 * a + 2)
                for qt, n in enumerate(QROWS):
                    sp.dma_start(att_d[a, qt * P:qt * P + n, :],
                                 oatt[0:n, par, qt, :, :].rearrange("p h d -> p (h d)")
                                 ).then_inc(att_saved[par], 16)

            def unit_b(u, par, k, b, g):
                if projects(k):
                    for t in range(KT):
                        load_ctx(u * KT + t, (par * KT + t) % 3, b * KT + t)
                        if t == KT - 1:
                            if k >= 2:
                                sp.wait_ge(s_ready, (u - 1) * NQ)
                            sp.dma_start(qT[:, par, :, :],
                                         qst_d[g, :, :, bass.ds(b * S, S)]).then_inc(q_in[par], 16)
                        if t == 2:
                            if k >= 2:
                                sp.wait_ge(gsum_ready, u * 2 - 2)
                            sp.dma_start(gbuf[:, par, :, :], wffn_d[u, :, :, :]).then_inc(gw_in[par], 16)
                if k == U:
                    load_ctx(U * KT, 0, 0)
                    sp.wait_ge(gsum_ready, 2 * U - 2)
                    sp.dma_start(gbuf[:, 0, :, :], wffn_d[U, :, :, :]).then_inc(gw_in[0], 16)
                if k >= 2:
                    save_att(u - 2, par)

            def prefetch_w(g):
                sp.wait_ge(wklo_ready, KC * g)
                sp.dma_start(wkraw[:, :, :], wkv_d[g, :, :, :]).then_inc(wk_in, 16)

            unit_b(0, 0, 0, 0, 0)
            prefetch_w(1)
            for u in range(1, 4):
                unit_b(u, u % 2, min(u, 2), u, 0)
            with sp.Fori(2, B // 2) as pair:
                for s in range(2):
                    unit_b(pair * 2 + s, s, 2, pair * 2 + s, 0)
            with sp.Fori(1, G - 1) as g:
                for s in range(2):
                    unit_b(g * B + s, s, 2, s, g)
                prefetch_w(g + 1)
                with sp.Fori(1, B // 2) as pair:
                    for s in range(2):
                        unit_b(g * B + pair * 2 + s, s, 2, pair * 2 + s, g)
            with sp.Fori(0, B // 2) as pair:
                for s in range(2):
                    unit_b((G - 1) * B + pair * 2 + s, s, 2, pair * 2 + s, G - 1)
            unit_b(U, 0, U, None, None)
            unit_b(U + 1, 1, U + 1, None, None)

            phase_b_over(sp)

            def load_l(i, s, b):
                sp.dma_start(cx[:, s, :], x_d.rearrange("i p d -> (i p) d")[bass.ds(i * LT, LT), :]
                             ).then_inc(lx_in[s], 16)
                for g in range(G):
                    sp.dma_start(ca[:, s, GC * g:GC * g + GC],
                                 att_d[g * B + b, LT * s:LT * s + LT, :]).then_inc(lx_in[s], 16)

            def save_x1(i, s):
                sp.wait_ge(x1_ready, i + 1)
                sp.dma_start(x1_d[bass.ds(i * LT, LT), :], ca[:, s, :]).then_inc(x1_saved[s], 16)

            for s in range(2):
                load_l(s, s, 0)
            with sp.Fori(1, B) as b:
                for s in range(2):
                    save_x1(b * 2 + (s - 2), s)
                    sp.wait_ge(x1_saved[s], b * 16)
                    sp.wait_ge(cn_ready, b * 2 + (s - 1))
                    load_l(b * 2 + s, s, b)
            for s in range(2):
                save_x1(NL - 2 + s, s)

            def load_w(j, s):
                for m in range(3):
                    sp.dma_start(wraw[:, s, m, :], wffn_d[m * (FJ // 2) + j, :, s, :]).then_inc(w_in[s], 16)

            for s in range(2):
                load_w(0, s)

            def save_hid(j, s):
                for c, (c0, n) in enumerate(CH):
                    sp.wait_ge(hl_ready, j * 4 + (c + 1))
                    sp.dma_start(hid_d[:, j, :, c0:c0 + n], hh[:, c % 2, :, 0:n]).then_inc(hid_saved[c % 2], 16)

            with sp.Fori(1, FJ // 2) as pair:
                for s in range(2):
                    sp.wait_ge(wquant_ready, pair * 6 + (3 * s - 3))
                    load_w(pair, s)
                    save_hid(pair * 2 + (s - 2), s)
            for s in range(2):
                save_hid(FJ - 2 + s, s)
            for s in range(2):
                sp.wait_ge(hid_saved[s], 32 * FJ)
                sp.wait_ge(x1_saved[s], 16 * B)

            def load_hid(m, par):
                sp.dma_start(hid[:, par, :, :, :], hid_d[:, :, :, bass.ds(m * MP, MP)]).then_inc(hid_in[par], 16)

            def load_x1(m, tt):
                sp.dma_start(x1b[:, tt, :], x1_d[bass.ds(m * MP + tt * P, P), :]).then_inc(x1_in[tt], 16)

            def save_out(m, tt):
                sp.wait_ge(ob_ready, m * 2 + tt + 1)
                sp.dma_start(out_d[bass.ds(m * MP + tt * P, P), :], ob[:, tt, :]).then_inc(out_saved[tt], 16)

            load_hid(0, 0)
            load_hid(1, 1)
            for tt in range(2):
                load_x1(0, tt)

            def step_d(m, par, more_x1, more_hid):
                if more_hid:
                    sp.wait_ge(y_ready, m * 2 + 2)
                    load_hid(m + 2, par)
                for tt in range(2):
                    save_out(m, tt)
                    if more_x1:
                        load_x1(m + 1, tt)

            step_d(0, 0, True, True)
            with sp.Fori(0, 2) as pair:
                for s in range(2):
                    step_d(pair * 2 + (s + 1), 1 - s, True, True)
            step_d(NM - 2, 1, True, False)
            step_d(NM - 1, 0, False, False)
            for tt in range(2):
                sp.wait_ge(out_saved[tt], 16 * NM)

        @block.gpsimd
        def _(pool):
            pool.memset(ident[:, :], 0.0).then_inc(pool_step, 1)
            pool.memset(identh[:, :], 0.0).then_inc(pool_step, 1)
            pool.memset(ones[:, :], 1.0).then_inc(consts_ready, 1)
            pool.memset(mhalf[:, :], -0.5).then_inc(consts_ready, 1)
            pool.memset(mone[:, :], -1.0).then_inc(consts_ready, 1)
            pool.memset(lneps[:, :], LN_EPS).then_inc(consts_ready, 1)
            pool.memset(rmseps[:, :], DH * RMS_EPS).then_inc(consts_ready, 1)
            pool.wait_ge(pool_step, 2)
            for m in (ident, identh):
                pool.affine_select(out=m[:, :], in_=m[:, :], compare_op=ALU.not_equal, fill=1.0, base=0,
                                   pattern=[[-1, P]], channel_multiplier=1).then_inc(consts_ready, 1)
            pool.wait_ge(consts_ready, 7)

            def x_rstd(i, par):
                pool.wait_ge(mv_ready, i + 1)
                wait(pool, xrs_ready, i)
                pool.tensor_tensor(vep[:, :], bag[:, par, 1:2], lneps[:, :], ALU.add).then_inc(vep_ready, 1)
                pool.wait_ge(vep_ready, i + 1)
                wait(pool, xn_ready, i - 1)
                pool.tensor_tensor(xrs[:, par, :], vep[:, :], mhalf[:, 0:1], ALU.pow).then_inc(xrs_ready, 1)

            def q_rstd(h):
                pool.wait_ge(qss_ready, h + 1)
                wait(pool, qrs_ready, h)
                pool.tensor_tensor(qms[:, :], qss[:, :], rmseps[:, :], ALU.add).then_inc(qms_ready, 1)
                pool.wait_ge(qms_ready, h + 1)
                wait(pool, qhat_ready, h)
                pool.tensor_tensor(qrs[:, :], qms[:, :], mhalf[:, :], ALU.pow).then_inc(qrs_ready, 1)

            x_rstd(0, 0)
            x_rstd(1, 1)

            def step_a(i, par, last):
                q_rstd(2 * i)
                q_rstd(2 * i + 1)
                if not last:
                    x_rstd(i + 2, par)

            tiles_of_x(pool, step_a)

            phase_a_over(pool)

            def k_rstd(T):
                pool.wait_ge(kss_ready, T + 1)
                wait(pool, krs_ready, T)
                pool.tensor_tensor(kms[0:KW, :], kss[0:KW, :], rmseps[0:KW, 0:HG], ALU.add
                                   ).then_inc(kms_ready, 1)
                pool.wait_ge(kms_ready, T + 1)
                wait(pool, khat_ready, T)
                pool.tensor_tensor(krs[0:KW, :], kms[0:KW, :], mhalf[0:KW, 0:HG], ALU.pow
                                   ).then_inc(krs_ready, 1)

            o_step = sem("o_step")

            def attend_out(a, par, qt):
                n = QROWS[qt]
                o = oraw[0:n, par, qt, :, :]
                done = a * 6 + 3 * qt
                if qt == 0:
                    pool.wait_ge(o_ready, a * 8 + 8)
                    wait(pool, att_saved[par], (a - par) * 16)
                wait(pool, att_ready, a * 2 + qt)
                pool.tensor_tensor(osum[0:n, :, :], o[:, :, 0:DH], o[:, :, 2 * DH:3 * DH], ALU.add
                                   ).then_inc(o_step, 1)
                pool.wait_ge(o_step, done + 1)
                pool.tensor_tensor(osum[0:n, :, :], osum[0:n, :, :], o[:, :, DH:2 * DH], ALU.add
                                   ).then_inc(o_step, 1)
                pool.tensor_tensor(oinv[0:n, :], o[:, :, 3 * DH], mone[0:n, :], ALU.pow).then_inc(o_step, 1)
                pool.wait_ge(o_step, done + 3)
                pool.tensor_tensor(oatt[0:n, par, qt, :, :], osum[0:n, :, :],
                                   oinv[0:n, :].unsqueeze(2).to_broadcast([n, HG, DH]), ALU.mult
                                   ).then_inc(att_ready, 1)

            def unit_b(u, par, k, b, g):
                for t in range(KT):
                    if behind(k, t, 1):
                        k_rstd(u * KT + (t - 1))
                    if k >= 2 and t in (3, 4):
                        attend_out(u - 2, par, t - 3)

            units(pool, unit_b)

            phase_b_over(pool)

            def l_rstd(i, s):
                pool.wait_ge(lmv_ready, i + 1)
                wait(pool, lrs_ready, i)
                pool.tensor_tensor(cve[:, :], cag[:, s, 1:2], lneps[0:LT, :], ALU.add).then_inc(lve_ready, 1)
                pool.wait_ge(lve_ready, i + 1)
                wait(pool, cn_ready, i - 1)
                pool.tensor_tensor(crs[:, s, :], cve[:, :], mhalf[0:LT, 0:1], ALU.pow).then_inc(lrs_ready, 1)

            for s in range(2):
                l_rstd(s, s)
            with pool.Fori(1, B) as b:
                for s in range(2):
                    l_rstd(b * 2 + s, s)

        @block.scalar
        def _(act):
            act.wait_ge(gates_in, 16)
            act.activation(tanhs[:, :], gates[:, :], ACT.Tanh).then_inc(tanh_ready, 1)

            def x_high(i, par):
                act.wait_ge(xT_ready, i + 1)
                wait(act, q_ready, 2 * (i - 1))
                act.activation(xhi[:, par, :], ps[:, 0:2, :].rearrange("p b n -> p (b n)"), ACT.Copy
                               ).then_inc(xhi_ready, 1)

            x_high(0, 0)
            for kc in range(KC):
                act.wait_ge(wq_in[kc % 4], 16 * (kc // 4 + 1))
                act.activation(wqhi[:, kc, :], wqraw[:, kc % 4, :], ACT.Copy).then_inc(wqhi_ready, 1)

            def w_high(g):
                act.wait_ge(wk_in, g * 16 + 16)
                if not isinstance(g, int):
                    act.wait_ge(kv_ready, g * (B * KT))
                for kc in range(KC):
                    act.activation(wkhi[:, kc, :], wkraw[:, kc, :], ACT.Copy).then_inc(wkhi_ready, 1)

            def half(h, c):
                b = 2 + c
                act.wait_ge(q_ready, h + 1)
                wait(act, qss_ready, h)
                act.activation(qsq[:, :, :], bank(b).rearrange("p (h d) -> p h d", d=DH), ACT.Square
                               ).then_inc(qsq_ready, 1)

            def half_high(h, c):
                act.wait_ge(qhat_ready, h + 1)
                wait(act, qT_ready, h - 1)
                act.activation(qnat[:, c, :, 0:4:2, :],
                               qhat[:, :, :].unsqueeze(2).to_broadcast([P, 16, 2, DH]), ACT.Copy
                               ).then_inc(qhi_ready, 1)

            def half_out(h, i, c):
                act.wait_ge(qT_ready, h + 1)
                if not isinstance(i, int) or i > 0:
                    act.wait_ge(q_saved[c], i * 32)
                act.activation(qTs[:, c, 0:8, :], bank(4 + 2 * c, F16).rearrange("p (h n) -> p h n", n=P),
                               ACT.Copy).then_inc(qTa_ready, 1)

            def step_a(i, par, last):
                first = isinstance(i, int) and i == 0
                for c in range(2):
                    h = 2 * i + c
                    half(h, c)
                    if c == 1 and (not last or last == NT - 2):
                        x_high(i + 1, 1 - par)
                    if not first:
                        half_out(h - 2, i - 1, c)
                    half_high(h, c)

            tiles_of_x(act, step_a)
            for c in range(2):
                half_out(2 * NT - 2 + c, NT - 1, c)

            w_high(0)
            phase_a_over(act)

            def ctx_high(T, par, slot, use):
                act.wait_ge(ctx_in[slot], use)
                wait(act, kv_ready, T - 1)
                act.activation(chi[:, par, :, :], craw[:, slot, :, :], ACT.Copy).then_inc(chi_ready, 1)

            ctx_high(0, 0, 0, 16)

            def group_b(g):
                if not isinstance(g, int):
                    w_high(g)

            def unit_b(u, par, k, b, g):
                for r in range(NQ):
                    t, j = r // 4, r % 4
                    Tb = u * KT + (t - 1)
                    pt = (par * KT + t - 1) % 2
                    vt = (t - 1) % KT
                    vp = par if t >= 1 else 1 - par

                    def value_high():
                        wait(act, pv_done, (u - 1) * NQ - 2 if t == 1 else (u - 1) * NQ if t > 1
                             else (u - 2) * NQ)
                        act.activation(val[0:KW, vp, vt, :, DH:2 * DH],
                                       bank(pt)[0:KW, GC:2 * GC].rearrange("p (h d) -> p h d", d=DH),
                                       ACT.Copy).then_inc(v1_ready, 1)

                    if j == 0 and behind(k, t, 1):
                        act.wait_ge(kv_ready, Tb + 1)
                        wait(act, kss_ready, Tb)
                        act.activation(ksq[0:KW, :, :],
                                       bank(pt)[0:KW, 0:GC].rearrange("p (h d) -> p h d", d=DH), ACT.Square
                                       ).then_inc(ksq_ready, 1)
                        if t != 1:
                            value_high()
                    if j == 1 and projects(k):
                        tn = par * KT + t + 1
                        slot = tn % 3
                        uses = (u - par) * 32 + 16 * (tn // 3 + 1)
                        ctx_high(u * KT + (t + 1), tn % 2, slot, uses)
                    if j == 3 and behind(k, t, 1):
                        act.wait_ge(vres_ready, Tb + 1)
                        act.activation(val[0:KW, vp, vt, :, 2 * DH:3 * DH], vres[0:KW, :, :], ACT.Copy
                                       ).then_inc(v2_ready, 1)
                        act.wait_ge(khat_ready, Tb + 1)
                        wait(act, kT_ready, Tb - 1)
                        act.activation(knat[0:KW, pt, :, 0:2, :],
                                       khat[0:KW, :, :].unsqueeze(2).to_broadcast([KW, HG, 2, DH]),
                                       ACT.Copy).then_inc(khi_ready, 1)
                    if r % 6 == 2 and attends(k, r, 14):
                        w = (r - 14) // 6
                        pr, op = (w % 4), (par if w < 0 else 1 - par)
                        act.wait_ge(pv_done, (u - 1) * NQ + 6 * w + 6)
                        if w == 0:
                            wait(act, att_ready, (u - 2) * 2)
                        for qt, n in enumerate(QROWS):
                            c0 = 2 * VW * qt
                            act.activation(oraw[0:n, op, qt, 2 * pr:2 * pr + 2, :],
                                           bank(6 + pr % 2)[0:n, c0:c0 + 2 * VW].rearrange(
                                               "p (h d) -> p h d", d=VW), ACT.Copy).then_inc(o_ready, 1)
                    if attends(k, r, SHIFT + 1):
                        e = r - SHIFT - 1
                        R = (u - 1) * NQ + e
                        act.wait_ge(p_ready, R + 1)
                        if not (k == 1 and e < 6):
                            act.wait_ge(pv_done, R - 5)
                        act.activation(phi[0:KW, e % 6, :, :],
                                       pf[0:KW, e % 6, :].rearrange("p (t n) -> p t n", t=2), ACT.Copy
                                       ).then_inc(phi_ready, 1)
                    if attends(k, r, SHIFT):
                        e = r - SHIFT
                        R = (u - 1) * NQ + e
                        act.wait_ge(s_ready, R + 1)
                        if not (k == 1 and e < 6):
                            act.wait_ge(plo_ready, R - 5)
                        act.activation(pf[0:KW, e % 6, :], bank(3 + e % 3)[0:KW, 0:2 * S], ACT.Exp,
                                       bias=LN128, scale=SCALE).then_inc(p_ready, 1)
                    if j == 1 and t == 1 and behind(k, t, 1):
                        value_high()

            units(act, unit_b, group_b)

            phase_b_over(act)

            def l_high(i, s):
                act.wait_ge(cn_ready, i + 1)
                if not isinstance(i, int):
                    act.wait_ge(cnT_ready, i - 1)
                act.activation(cnh[:, s, :], cn[:, s, :], ACT.Copy).then_inc(cnh_ready, 1)

            def l_out(i, s):
                act.wait_ge(cnT_ready, i + 1)
                act.activation(xnTh[:, :, bass.ds(i * LT, LT)],
                               bank(4 + 2 * s, F16).rearrange("p (k n) -> p k n", n=P)[:, :, 0:LT], ACT.Copy
                               ).then_inc(xnTh_ready, 1)

            for s in range(2):
                l_high(s, s)
            with act.Fori(1, B) as b:
                for s in range(2):
                    l_out(b * 2 + (s - 2), s)
                    l_high(b * 2 + s, s)
            for s in range(2):
                l_out(NL - 2 + s, s)

            def hidden(j, first):
                for c, (c0, n) in enumerate(CH):
                    m = j * 4 + c
                    act.wait_ge(h_ready, m + 1)
                    wait(act, hf_ready, m - 1)
                    act.activation(sg[:, c % 2, 0:n], bank(c % 2)[:, 0:n], ACT.Sigmoid).then_inc(sg_ready, 1)
                    act.wait_ge(hf_ready, m + 1)
                    if not (first and c < 2):
                        act.wait_ge(hid_saved[c % 2], j * 32 + 16 * (c // 2))
                    act.activation(hh[:, c % 2, 0, 0:n], hf[:, c % 2, 0:n], ACT.Copy).then_inc(hh_ready, 1)

            hidden(0, True)
            with act.Fori(1, FJ) as j:
                hidden(j, False)

        @block.vector
        def _(dve):
            def x_norm(i, par):
                dve.wait_ge(x_in[par], (i - par) * 8 + 16)
                wait(dve, mv_ready, i)
                wait(dve, xn_ready, i - 1)
                for c in range(2):
                    dve.bn_stats(bst[:, c, :], xraw[:, par, 512 * c:512 * c + 512])
                dve.drain()
                dve.bn_aggr(bag[:, par, :], bst[:, :, :]).then_inc(mv_ready, 1)

            def x_norm2(i, par):
                dve.wait_ge(xrs_ready, i + 1)
                wait(dve, xT_ready, i)
                dve.tensor_scalar(xn[:, :], xraw[:, par, :], bag[:, par, 0:1], xrs[:, par, :], ALU.subtract,
                                  ALU.mult).then_inc(xn_ready, 1)

            def x_low(i, par):
                dve.wait_ge(xhi_ready, i + 1)
                dve.tensor_tensor(xlo[:, par, :], ps[:, 0:2, :].rearrange("p b n -> p (b n)"),
                                  xhi[:, par, :].bitcast(F32), ALU.subtract).then_inc(xlo_ready, 1)

            x_norm(0, 0)
            x_norm(1, 1)
            x_norm2(0, 0)
            x_low(0, 0)
            for kc in range(KC):
                dve.wait_ge(wqhi_ready, kc + 1)
                dve.tensor_tensor(wqlo[:, kc, :], wqraw[:, kc % 4, :], wqhi[:, kc, :].bitcast(F32),
                                  ALU.subtract).then_inc(wqlo_ready, 1)
            x_norm2(1, 1)

            def half_sums(h):
                dve.wait_ge(qsq_ready, h + 1)
                wait(dve, qrs_ready, h)
                dve.tensor_reduce(qss[:, :], qsq[:, :, :], AX_X, ALU.add).then_inc(qss_ready, 1)

            def half_norm(h, c):
                dve.wait_ge(qrs_ready, h + 1)
                wait(dve, qlo_ready, h)
                dve.scalar_tensor_tensor(out=qhat[:, :, :], in0=bank(2 + c).rearrange("p (h d) -> p h d", d=DH),
                                         scalar=ROOT, in1=qrs[:, :].unsqueeze(2).to_broadcast([P, 16, DH]),
                                         op0=ALU.mult, op1=ALU.mult).then_inc(qhat_ready, 1)

            def half_low(h, c):
                dve.wait_ge(qhi_ready, h + 1)
                dve.tensor_tensor(qnat[:, c, :, 1:4:2, :],
                                  qhat[:, :, :].unsqueeze(2).to_broadcast([P, 16, 2, DH]),
                                  qnat[:, c, :, 0:4:2, :], ALU.subtract).then_inc(qlo_ready, 1)

            def half_out(h, i, c):
                dve.wait_ge(qT_ready, h + 1)
                if not isinstance(i, int) or i > 0:
                    dve.wait_ge(q_saved[c], i * 32)
                dve.tensor_copy(qTs[:, c, 8:16, :], bank(5 + 2 * c, F16).rearrange("p (h n) -> p h n", n=P)
                                ).then_inc(qTb_ready, 1)

            def step_a(i, par, last):
                first = isinstance(i, int) and i == 0
                for c in range(2):
                    h = 2 * i + c
                    half_sums(h)
                    if not (first and c == 0):
                        half_low(h - 1, 1 - c)
                    if c == 1 and (not last or last == NT - 2):
                        x_low(i + 1, 1 - par)
                    if not first:
                        half_out(h - 2, i - 1, c)
                    if c == 1 and not last:
                        x_norm(i + 2, par)
                    half_norm(h, c)
                if not last:
                    x_norm2(i + 2, par)

            tiles_of_x(dve, step_a)
            half_low(2 * NT - 1, 1)
            for c in range(2):
                half_out(2 * NT - 2 + c, NT - 1, c)

            def w_low(g):
                for kc in range(KC):
                    dve.wait_ge(wkhi_ready, g * KC + (kc + 1))
                    dve.tensor_tensor(wklo[:, kc, :], wkraw[:, kc, :], wkhi[:, kc, :].bitcast(F32),
                                      ALU.subtract).then_inc(wklo_ready, 1)

            w_low(0)
            phase_a_over(dve)
            dve.memset(val[:, :, :, :, 3 * DH:VW], 1.0).then_inc(v3_ready, 1)

            def ctx_low(T, par, slot):
                dve.wait_ge(chi_ready, T + 1)
                dve.tensor_tensor(clo[:, par, :, :], craw[:, slot, :, :], chi[:, par, :, :].bitcast(F32),
                                  ALU.subtract).then_inc(clo_ready, 1)

            ctx_low(0, 0, 0)

            def group_b(g):
                if not isinstance(g, int):
                    w_low(g)

            def unit_b(u, par, k, b, g):
                for r in range(NQ):
                    t, j = r // 4, r % 4
                    Tb = u * KT + (t - 1)
                    pt = (par * KT + t - 1) % 2
                    vt = (t - 1) % KT
                    vp = par if t >= 1 else 1 - par
                    if j == 0 and behind(k, t, 2):
                        dve.wait_ge(khi_ready, Tb)
                        dve.tensor_tensor(knat[0:KW, 1 - pt, :, 2:4, :],
                                          khat[0:KW, :, :].unsqueeze(2).to_broadcast([KW, HG, 2, DH]),
                                          knat[0:KW, 1 - pt, :, 0:2, :], ALU.subtract).then_inc(klo_ready, 1)
                    if j == 0 and behind(k, t, 1):
                        dve.wait_ge(ksq_ready, Tb + 1)
                        wait(dve, krs_ready, Tb)
                        dve.tensor_reduce(kss[0:KW, :], ksq[0:KW, :, :], AX_X, ALU.add).then_inc(kss_ready, 1)
                    if j == (2 if t == 1 else 1) and behind(k, t, 1):
                        dve.wait_ge(v1_ready, Tb + 1)
                        if k or t > 1:
                            dve.wait_ge(v3_ready, Tb + 1)
                        dve.tensor_tensor(vres[0:KW, :, :],
                                          bank(pt)[0:KW, GC:2 * GC].rearrange("p (h d) -> p h d", d=DH),
                                          val[0:KW, vp, vt, :, DH:2 * DH], ALU.subtract
                                          ).then_inc(vres_ready, 1)
                    if j == 1 and projects(k):
                        tn = par * KT + t + 1
                        ctx_low(u * KT + (t + 1), tn % 2, tn % 3)
                    if j == 2 and behind(k, t, 1):
                        dve.wait_ge(krs_ready, Tb + 1)
                        wait(dve, klo_ready, Tb)
                        dve.scalar_tensor_tensor(
                            out=khat[0:KW, :, :], in0=bank(pt)[0:KW, 0:GC].rearrange("p (h d) -> p h d", d=DH),
                            scalar=ROOT, in1=krs[0:KW, :].unsqueeze(2).to_broadcast([KW, HG, DH]),
                            op0=ALU.mult, op1=ALU.mult).then_inc(khat_ready, 1)
                    if j == 2 and behind(k, t, 2):
                        tt = (t - 2) % KT
                        kp = par if t >= 2 else 1 - par
                        dve.wait_ge(kT_ready, Tb)
                        wait(dve, s_ready, (u - 1) * NQ if t >= 2 else (u - 2) * NQ)
                        dve.tensor_copy(kst[:, kp, :, tt * KW:tt * KW + KW],
                                        bank(2, F16).rearrange("p (h n) -> p h n", n=P)[:, :, 0:KW]
                                        ).then_inc(kst_ready, 1)
                    if j == 3 and behind(k, t, 1):
                        dve.wait_ge(v2_ready, Tb + 1)
                        dve.tensor_tensor(val[0:KW, vp, vt, :, 0:DH], vres[0:KW, :, :],
                                          val[0:KW, vp, vt, :, 2 * DH:3 * DH], ALU.subtract
                                          ).then_inc(v3_ready, 1)
                    if r in (7, 15) and k <= U:
                        a = r // 8
                        if a == 0:
                            dve.wait_ge(gw_in[par], (u - par) * 8 + 16)
                        dve.tensor_reduce(gsum[:, bass.ds(u * 2 + a, 1)], gbuf[:, par, a, :], AX_X, ALU.add,
                                          apply_absolute_value=True).then_inc(gsum_ready, 1)
                    if attends(k, r, SHIFT + 1):
                        e = r - SHIFT - 1
                        dve.wait_ge(phi_ready, (u - 1) * NQ + e + 1)
                        dve.tensor_tensor(plo[0:KW, e % 6, :, :],
                                          pf[0:KW, e % 6, :].rearrange("p (t n) -> p t n", t=2),
                                          phi[0:KW, e % 6, :, :], ALU.subtract).then_inc(plo_ready, 1)

            units(dve, unit_b, group_b)

            dve.wait_ge(gsum_ready, 2 * WPAIRS)
            dve.tensor_reduce(gmat[:, :], gsum[:, :].rearrange("p (m n) -> p m n", m=3), AX_X, ALU.add
                              ).then_inc(gmat_ready, 1)
            dve.wait_ge(gall_ready, 1)
            dve.tensor_scalar(thr[:, 0, :], bank(0)[:, 0:3], 1.0 / (F * D), Q_EPS, ALU.mult, ALU.add
                              ).then_inc(thr_step, 1)
            dve.wait_ge(thr_step, 1)
            dve.tensor_scalar(thr[:, 1, :], thr[:, 0, :], 0.5, None, ALU.mult).then_inc(thr_step, 1)
            dve.tensor_scalar(thr[:, 2, :], thr[:, 0, :], -0.5, None, ALU.mult).then_inc(thr_step, 1)
            dve.wait_ge(thr_step, 3)
            dve.wait_ge(tanh_ready, 1)

            phase_b_over(dve)

            def l_sum(i, s):
                dve.wait_ge(lx_in[s], (i - s) * 40 + 80)
                dve.scalar_tensor_tensor(out=ca[:, s, :], in0=ca[:, s, :], scalar=tanhs[0:LT, 0:1],
                                         in1=cx[:, s, :], op0=ALU.mult, op1=ALU.add).then_inc(x1_ready, 1)
                dve.wait_ge(x1_ready, i + 1)
                wait(dve, lmv_ready, i)
                wait(dve, cn_ready, i - 1)
                for c in range(2):
                    dve.bn_stats(cst[:, c, :], ca[:, s, 512 * c:512 * c + 512])
                dve.drain()
                dve.bn_aggr(cag[:, s, :], cst[:, :, :]).then_inc(lmv_ready, 1)

            def l_norm(i, s):
                dve.wait_ge(lrs_ready, i + 1)
                if not isinstance(i, int):
                    dve.wait_ge(cnl_ready, i - 1)
                dve.tensor_scalar(cn[:, s, :], ca[:, s, :], cag[:, s, 0:1], crs[:, s, :], ALU.subtract,
                                  ALU.mult).then_inc(cn_ready, 1)

            def l_low(i, s):
                dve.wait_ge(cnh_ready, i + 1)
                if not isinstance(i, int):
                    dve.wait_ge(cnT_ready, i - 1)
                dve.tensor_tensor(cnl[:, s, :], cn[:, s, :], cnh[:, s, :], ALU.subtract).then_inc(cnl_ready, 1)

            def l_out(i, s):
                dve.wait_ge(cnT_ready, i + 1)
                dve.tensor_copy(xnTl[:, :, bass.ds(i * LT, LT)],
                                bank(5 + 2 * s, F16).rearrange("p (k n) -> p k n", n=P)[:, :, 0:LT]
                                ).then_inc(xnTl_ready, 1)

            for s in range(2):
                l_sum(s, s)
                l_norm(s, s)
                l_low(s, s)
            with dve.Fori(1, B) as b:
                for s in range(2):
                    l_sum(b * 2 + s, s)
                    l_out(b * 2 + (s - 2), s)
                    l_norm(b * 2 + s, s)
                    l_low(b * 2 + s, s)
            for s in range(2):
                l_out(NL - 2 + s, s)

            def quantise(j, pair, s):
                dve.wait_ge(w_in[s], pair * 48 + 48)
                for m in range(3):
                    n = j * 3 + m
                    wait(dve, wquant_ready, n)
                    dve.tensor_scalar(wneg[:, :], wraw[:, s, m, :], thr[:, 2, m:m + 1], None, ALU.is_lt
                                      ).then_inc(wneg_ready, 1)
                    dve.wait_ge(wneg_ready, n + 1)
                    if m < 2:
                        if m == 0:
                            wait(dve, h_ready, (j - 1) * 4)
                        dst = w12q[:, s, m, :, :].rearrange("p k n -> p (k n)")
                    else:
                        dst = w3q[:, j, :]
                    dve.scalar_tensor_tensor(out=dst, in0=wraw[:, s, m, :], scalar=thr[:, 1, m:m + 1],
                                             in1=wneg[:, :], op0=ALU.is_gt, op1=ALU.subtract
                                             ).then_inc(wquant_ready, 1)

            def hidden(j, first):
                for c, (c0, n) in enumerate(CH):
                    m = j * 4 + c
                    dve.wait_ge(sg_ready, m + 1)
                    if not (first and c < 2):
                        dve.wait_ge(hl_ready, m - 1)
                    dve.tensor_tensor(hf[:, c % 2, 0:n], bank(2 + c % 2)[:, 0:n], sg[:, c % 2, 0:n], ALU.mult
                                      ).then_inc(hf_ready, 1)
                    dve.wait_ge(hh_ready, m + 1)
                    dve.tensor_tensor(hh[:, c % 2, 1, 0:n], hf[:, c % 2, 0:n], hh[:, c % 2, 0, 0:n],
                                      ALU.subtract).then_inc(hl_ready, 1)

            quantise(0, 0, 0)
            quantise(1, 0, 1)
            hidden(0, True)
            with dve.Fori(1, FJ // 2) as pair:
                quantise(pair * 2, pair, 0)
                hidden(pair * 2 - 1, False)
                quantise(pair * 2 + 1, pair, 1)
                hidden(pair * 2, False)
            hidden(FJ - 1, False)

            def result(m, par, first):
                for tt in range(2):
                    dve.wait_ge(y_ready, m * 2 + tt + 1)
                    dve.wait_ge(x1_in[tt], m * 16 + 16)
                    if not first:
                        dve.wait_ge(out_saved[tt], m * 16)
                    b0 = 4 * par + 2 * tt
                    dve.scalar_tensor_tensor(out=ob[:, tt, :], in0=ps[:, b0:b0 + 2, :].rearrange("p b n -> p (b n)"),
                                             scalar=tanhs[:, 1:2], in1=x1b[:, tt, :], op0=ALU.mult,
                                             op1=ALU.add).then_inc(ob_ready, 1)

            result(0, 0, True)
            with dve.Fori(0, NM // 2) as pair:
                result(pair * 2 + 1, 1, False)
                result(pair * 2 + 2, 0, False)

        @block.tensor
        def _(pe):
            pe.wait_ge(consts_ready, 7)

            def x_transpose(i):
                pe.wait_ge(xn_ready, i + 1)
                wait(pe, xlo_ready, i)
                for kc in range(KC):
                    mm = pe.transpose(ps[:, kc // 4, (kc % 4) * P:(kc % 4) * P + P],
                                      xn[:, kc * P:kc * P + P], ident[:, :])
                mm.then_inc(xT_ready, 1)

            def q_half(h, i, par, c, first):
                pe.wait_ge(xlo_ready, i + 1)
                wait(pe, qhat_ready, h - 1)
                for kc in range(KC):
                    if first:
                        pe.wait_ge(wqlo_ready, kc + 1)
                    cols = slice(512 * c, 512 * c + 512)
                    for n, (a, w) in enumerate(((xhi, wqhi), (xhi, wqlo), (xlo, wqhi))):
                        mm = pe.matmul(bank(2 + c), a[:, par, kc * P:kc * P + P], w[:, kc, cols],
                                       start=(kc == 0 and n == 0), stop=(kc == KC - 1 and n == 2))
                mm.then_inc(q_ready, 1)

            def q_stack(h, c):
                pe.wait_ge(qlo_ready, h + 1)
                wait(pe, qTa_ready, h - 1)
                wait(pe, qTb_ready, h - 1)
                for n in range(16):
                    b = 4 + 2 * c + n // 8
                    mm = pe.transpose(bank(b, F16)[:, (n % 8) * P:(n % 8) * P + P],
                                      qnat[:, c, n, :, :].rearrange("p a d -> p (a d)"), identh[:, :])
                mm.then_inc(qT_ready, 1)

            x_transpose(0)

            def step_a(i, par, last):
                first = isinstance(i, int) and i == 0
                for c in range(2):
                    q_half(2 * i + c, i, par, c, first and c == 0)
                    if not first:
                        q_stack(2 * i - 2 + c, c)
                    if c == 0 and (not last or last == NT - 2):
                        x_transpose(i + 1)

            tiles_of_x(pe, step_a)
            for c in range(2):
                q_stack(2 * NT - 2 + c, c)

            phase_a_over(pe)
            pe.wait_ge(v3_ready, 1)

            def unit_b(u, par, k, b, g):
                for r in range(NQ):
                    t, j = r // 4, r % 4
                    T = u * KT + t
                    pt = (par * KT + t) % 2
                    if projects(k):
                        if j == 0:
                            pe.wait_ge(clo_ready, T + 1)
                            if k >= 1 or t >= 2:
                                wait(pe, khat_ready, T - 1)
                                wait(pe, vres_ready, T - 1)
                        for kc in (2 * j, 2 * j + 1):
                            if t == 0 and par == 0 and (k == 0 or not isinstance(g, int)):
                                pe.wait_ge(wklo_ready, g * KC + (kc + 1))
                            for n, (a, w) in enumerate(((chi, wkhi), (chi, wklo), (clo, wkhi))):
                                mm = pe.matmul(bank(pt)[0:KW, :], a[:, pt, kc, :], w[:, kc, :],
                                               start=(kc == 0 and n == 0), stop=(kc == KC - 1 and n == 2))
                        if j == 3:
                            mm.then_inc(kv_ready, 1)
                    if attends(k, r, SHIFT):
                        e = r - SHIFT
                        ap = 1 - par if e >= 0 else par
                        hd, c = (e % NQ) // 3, e % 3
                        R = (u - 1) * NQ + e
                        if e in (0, 1, 2):
                            pe.wait_ge(kst_ready, (u - 1) * KT + 2 * c + 2)
                        if e == 0:
                            pe.wait_ge(q_in[ap], (u - 1 - ap) * 8 + 16)
                        if not (k == 1 and e < 3):
                            pe.wait_ge(p_ready, R - 2)
                        for n in range(2):
                            kt = 2 * c + n
                            mm = pe.matmul(bank(3 + e % 3)[0:KW, S * n:S * n + S],
                                           kst[:, ap, hd, KW * kt:KW * kt + KW], qT[:, ap, hd, :],
                                           start=True, stop=True)
                        mm.then_inc(s_ready, 1)
                    if attends(k, r, SHIFT + LAG):
                        e = r - SHIFT - LAG
                        ap = 1 - par if e >= 0 else par
                        hd, c = (e % NQ) // 3, e % 3
                        R = (u - 1) * NQ + e
                        sl = e % 6
                        pair = hd // 2
                        if e == 0:
                            pe.wait_ge(v3_ready, u * KT + 1)
                        if e % 6 == 0 and not (k == 1 and e < 12):
                            pe.wait_ge(o_ready, (u - 1) * 8 + 2 * (e // 6) - 2)
                        pe.wait_ge(plo_ready, R + 1)
                        for qt, nq in enumerate(QROWS):
                            c0 = 2 * VW * qt + VW * (hd % 2)
                            o = bank(6 + pair % 2)
                            for n in range(2):
                                kt = 2 * c + n
                                q = slice(P * qt, P * qt + nq)
                                mm = pe.matmul(o[0:nq, c0:c0 + VW], phi[0:KW, sl, n, q], val[0:KW, ap, kt, hd, :],
                                               start=(e % 6 == 0 and qt == 0 and n == 0), stop=False,
                                               skip_group_check=True)
                                mm = pe.matmul(o[0:nq, c0 + DH:c0 + VW], plo[0:KW, sl, n, q],
                                               val[0:KW, ap, kt, hd, DH:VW], start=False,
                                               stop=(e % 6 == 5 and n == 1), skip_group_check=True)
                        mm.then_inc(pv_done, 1)
                    if j == 1 and behind(k, t, 2):
                        pn = pt
                        pe.wait_ge(klo_ready, T - 1)
                        wait(pe, kst_ready, T - 2)
                        for h in range(HG):
                            mm = pe.transpose(bank(2, F16)[:, h * P:h * P + KW],
                                              knat[0:KW, pn, h, :, :].rearrange("p a d -> p (a d)"),
                                              identh[0:KW, 0:KW])
                        mm.then_inc(kT_ready, 1)

            units(pe, unit_b)

            pe.wait_ge(gmat_ready, 1)
            pe.matmul(bank(0)[:, 0:3], ones[:, :], gmat[:, :], start=True, stop=True).then_inc(gall_ready, 1)

            phase_b_over(pe)

            def l_transpose(i, s):
                pe.wait_ge(cnl_ready, i + 1)
                if not isinstance(i, int):
                    pe.wait_ge(xnTh_ready, i - 1)
                    pe.wait_ge(xnTl_ready, i - 1)
                for part, src in enumerate((cnh, cnl)):
                    for kc in range(KC):
                        mm = pe.transpose(bank(4 + 2 * s + part, F16)[:, kc * P:kc * P + LT],
                                          src[:, s, kc * P:kc * P + P], identh[0:LT, 0:LT])
                mm.then_inc(cnT_ready, 1)

            for s in range(2):
                l_transpose(s, s)
            with pe.Fori(1, B) as b:
                for s in range(2):
                    l_transpose(b * 2 + s, s)

            def hidden(j, s, first):
                if first:
                    pe.wait_ge(thr_step, 3)
                pe.wait_ge(wquant_ready, j * 3 + 2)
                for c, (c0, n) in enumerate(CH):
                    if first:
                        pe.wait_ge(xnTh_ready, -(-(c0 + n) // LT))
                        pe.wait_ge(xnTl_ready, -(-(c0 + n) // LT))
                    if not (first and c < 2):
                        pe.wait_ge(hf_ready, j * 4 + c - 1)
                    for m in range(2):
                        o = bank(2 * m + c % 2)[:, 0:n]
                        for kc in range(KC):
                            for part, xt in enumerate((xnTh, xnTl)):
                                mm = pe.matmul(o, w12q[:, s, m, kc, :], xt[:, kc, c0:c0 + n],
                                               start=(kc == 0 and part == 0), stop=(kc == KC - 1 and part == 1))
                    mm.then_inc(h_ready, 1)

            hidden(0, 0, True)
            hidden(1, 1, False)
            with pe.Fori(1, FJ // 2) as pair:
                for s in range(2):
                    hidden(pair * 2 + s, s, False)

            pe.wait_ge(wquant_ready, 3 * FJ)
            pe.wait_ge(hf_ready, 4 * FJ)

            def result(m, par, first):
                pe.wait_ge(hid_in[par], (m - par) * 8 + 16)
                for tt in range(2):
                    if not first:
                        pe.wait_ge(ob_ready, m * 2 + tt - 3)
                    for c in range(2):
                        for j in range(FJ):
                            for part in range(2):
                                mm = pe.matmul(bank(4 * par + 2 * tt + c),
                                               hid[:, par, j, part, P * tt:P * tt + P],
                                               w3q[:, j, 512 * c:512 * c + 512],
                                               start=(j == 0 and part == 0), stop=(j == FJ - 1 and part == 1))
                    mm.then_inc(y_ready, 1)

            result(0, 0, True)
            result(1, 1, True)
            result(2, 0, False)
            with pe.Fori(1, NM // 2) as pair:
                result(pair * 2 + 1, 1, False)
                result(pair * 2 + 2, 0, False)


def kernel(x, ctx_2048, g_xattn, g_ffn, L0_xattn_Wq, L0_xattn_Wk, L0_xattn_Wv, L0_ffn_w1, L0_ffn_w2, L0_ffn_w3):
    import numpy as np
    import concourse.bacc as bacc
    from concourse.bass_utils import run_bass_kernel_spmd

    def c(a):
        return np.ascontiguousarray(a)

    wkv = np.concatenate([np.asarray(L0_xattn_Wk), np.asarray(L0_xattn_Wv)], axis=0)
    wkv = wkv.reshape(G, GC, 2, KC, P).transpose(0, 4, 3, 2, 1).reshape(G, P, KC, 512)
    w12 = [np.asarray(w).reshape(FJ, P, KC, P).transpose(0, 3, 2, 1).reshape(FJ, P, D)
           for w in (L0_ffn_w1, L0_ffn_w2)]
    w3 = np.asarray(L0_ffn_w3).T.reshape(FJ, P, D)
    wffn = np.stack([*w12, w3]).reshape(WPAIRS, 2, P, D).transpose(0, 2, 1, 3)
    arrays = {
        "in_x": c(np.asarray(x).reshape(NT, P, D)),
        "in_ctx": c(np.asarray(ctx_2048).reshape(B * KT, KW, KC, P).transpose(0, 3, 2, 1)),
        "in_wq": c(np.asarray(L0_xattn_Wq).reshape(D, KC, P).transpose(2, 1, 0)),
        "in_wkv": c(wkv),
        "in_wffn": c(wffn),
        "in_gates": c(np.broadcast_to(np.concatenate([np.asarray(g_xattn), np.asarray(g_ffn)])[None, :], (P, 2))),
    }
    nc = bacc.Bacc("TRN2", target_bir_lowering=False, num_devices=1)
    args = [nc.dram_tensor(n, a.shape, F32, kind="ExternalInput").ap() for n, a in arrays.items()]
    out = nc.dram_tensor("out", (TOK, D), F32, kind="ExternalOutput").ap()
    flamingo_kernel(nc, *args, out)
    r = run_bass_kernel_spmd(nc, [arrays], core_ids=[0])
    return r.results[0]["out"].reshape(B, S, D)
```

```python
from contextlib import ExitStack

import concourse.bass as bass
from concourse import mybir

ALU = mybir.AluOpType
ACT = mybir.ActivationFunctionType
AX_X = mybir.AxisListType.X
F32 = mybir.dt.float32
F32R = mybir.dt.float32r
F16 = mybir.dt.float16
BF16 = mybir.dt.bfloat16

P = 128
B, S, D = 8, 224, 1024
SK = 750
DH = 32
F = 2816
KC = D // P
TOK = B * S
NT = TOK // P
KT, KW = 6, 125
G, HG = 4, 8
GC = HG * DH
U = G * B
NQ = 4 * KT
VW = 3 * DH + 1
SHIFT = 5
LAG = 3
LNLAG = 3
QROWS = (P, S - P)
LT = 112
NL = TOK // LT
FJ = F // P
CH = ((0, 512), (512, 512), (1024, 512), (1536, 256))
MP = 2 * P
NM = TOK // MP
WPAIRS = 3 * FJ // 2
LN_EPS, RMS_EPS, Q_EPS = 1e-5, 1e-6, 1e-8
SCALE = float(DH) ** -0.5
ROOT = float(DH) ** 0.5
LN128 = 4.852030263919617


def wait(eng, sem, n):
    if not isinstance(n, int) or n > 0:
        eng.wait_ge(sem, n)


def flamingo_kernel(nc, x_d, ctx_d, wq_d, wkv_d, wffn_d, gates_d, out_d):
    qst_d = nc.dram_tensor("q_stacks", [G, P, HG, TOK], F16, kind="Internal").ap()
    att_d = nc.dram_tensor("attention", [U, S, GC], F32, kind="Internal").ap()
    cn_d = nc.dram_tensor("x1_normalised", [TOK, 2, D], F16, kind="Internal").ap()
    x1_d = nc.dram_tensor("x_after_attention", [TOK, D], F32, kind="Internal").ap()
    hid_d = nc.dram_tensor("hidden", [P, FJ, 2, TOK], F16, kind="Internal").ap()

    top = ExitStack()

    def sem(name):
        return top.enter_context(nc.semaphore(name))

    def sb(scope, name, shape, dt):
        return scope.enter_context(nc.sbuf_tensor(name, shape, dt))

    with top:
        ident = sb(top, "ident", [P, P], F32)
        identh = sb(top, "identh", [P, P], F16)
        ones = sb(top, "ones", [P, P], F32)
        mhalf = sb(top, "mhalf", [P, 16], F32)
        mone = sb(top, "mone", [P, HG], F32)
        lneps = sb(top, "lneps", [P, 1], F32)
        rmseps = sb(top, "rmseps", [P, 16], F32)
        gates = sb(top, "gates", [P, 2], F32)
        tanhs = sb(top, "tanhs", [P, 2], F32)
        gsum = sb(top, "gsum", [P, 2 * WPAIRS], F32)
        gmat = sb(top, "gmat", [P, 3], F32)
        thr = sb(top, "thr", [P, 3, 3], F32)
        oraw = sb(top, "oraw", [P, 2, 2, HG, VW], F32)
        osum = sb(top, "osum", [P, HG, DH], F32)
        oinv = sb(top, "oinv", [P, HG], F32)
        oatt = sb(top, "oatt", [P, 2, 2, HG, DH], F32)
        cst = sb(top, "cst", [LT, 2, 6], F32)
        cag = sb(top, "cag", [LT, 4, 2], F32)
        cve = sb(top, "cve", [LT, 1], F32)
        crs = sb(top, "crs", [LT, 4, 1], F32)
        ps = top.enter_context(nc.psum_tensor("ps", [P, 8, 512], F32))

        def bank(b, dt=F32):
            v = ps[:, b, :]
            return v if dt == F32 else v.bitcast(dt)

        ab = ExitStack()
        wkhi = sb(ab, "wkhi", [P, KC, 512], F32R)
        wklo = sb(ab, "wklo", [P, KC, 512], F32R)
        wkraw = sb(ab, "wkraw", [P, KC, 512], F32)

        pa = ExitStack()
        wqraw = sb(pa, "wqraw", [P, 4, D], F32)
        wqhi = sb(pa, "wqhi", [P, KC, D], F32R)
        wqlo = sb(pa, "wqlo", [P, KC, D], F32R)
        xraw = sb(pa, "xraw", [P, 2, D], F32)
        xn = sb(pa, "xn", [P, D], F32)
        xhi = sb(pa, "xhi", [P, 2, D], F32R)
        xlo = sb(pa, "xlo", [P, 2, D], F32R)
        qsq = sb(pa, "qsq", [P, 16, DH], F32)
        qhat = sb(pa, "qhat", [P, 16, DH], F32)
        qnat = sb(pa, "qnat", [P, 2, 16, 4, DH], F16)
        qTs = sb(pa, "qTs", [P, 2, 16, P], F16)
        bst = sb(pa, "bst", [P, 2, 6], F32)
        bag = sb(pa, "bag", [P, 2, 2], F32)
        vep = sb(pa, "vep", [P, 1], F32)
        xrs = sb(pa, "xrs", [P, 2, 1], F32)
        qss = sb(pa, "qss", [P, 16], F32)
        qms = sb(pa, "qms", [P, 16], F32)
        qrs = sb(pa, "qrs", [P, 16], F32)
        pa.close()

        pb = ExitStack()
        craw = sb(pb, "craw", [P, 3, KC, KW], F32)
        chi = sb(pb, "chi", [P, 2, KC, KW], F32R)
        clo = sb(pb, "clo", [P, 2, KC, KW], F32R)
        kst = sb(pb, "kst", [P, 2, HG, SK], F16)
        val = sb(pb, "val", [P, 2, KT, HG, VW], BF16)
        qT = sb(pb, "qT", [P, 2, HG, S], F16)
        pf = sb(pb, "pf", [P, 6, 2 * S], F32)
        phi = sb(pb, "phi", [P, 6, 2, S], F16)
        plo = sb(pb, "plo", [P, 6, 2, S], F16)
        ksq = sb(pb, "ksq", [P, HG, DH], F32)
        khat = sb(pb, "khat", [P, HG, DH], F32)
        knat = sb(pb, "knat", [P, 2, HG, 4, DH], F16)
        vres = sb(pb, "vres", [P, HG, DH], F32)
        kss = sb(pb, "kss", [P, HG], F32)
        kms = sb(pb, "kms", [P, HG], F32)
        krs = sb(pb, "krs", [P, HG], F32)
        gbuf = sb(pb, "gbuf", [P, 2, 2, D], F32)
        pb.close()
        ab.close()

        def ln_slot_memory(scope, n):
            return (sb(scope, f"cx{n}", [LT, D], F32), sb(scope, f"ca{n}", [LT, D], F32),
                    sb(scope, f"cn{n}", [LT, 2, D], F16))

        ln_mem = {2: ln_slot_memory(top, 2), 3: ln_slot_memory(top, 3)}
        early = ExitStack()
        ln_mem[1] = ln_slot_memory(early, 1)
        ln_mem[0] = ln_slot_memory(early, 0)
        early.close()

        w3q = sb(top, "w3q", [P, FJ, D], BF16)
        pc = ExitStack()
        xnTh = sb(pc, "xnTh", [P, KC, TOK], F16)
        xnTl = sb(pc, "xnTl", [P, KC, TOK], F16)
        stage = sb(pc, "stage", [LT, 4, 2, D], F16)
        wraw = sb(pc, "wraw", [P, 2, 3, D], F32)
        wneg = sb(pc, "wneg", [P, D], BF16)
        w12q = sb(pc, "w12q", [P, 2, 2, KC, P], BF16)
        sg = sb(pc, "sg", [P, 2, 512], F32)
        hf = sb(pc, "hf", [P, 2, 512], F32)
        hh = sb(pc, "hh", [P, 2, 2, 512], F16)
        pc.close()
        pd = ExitStack()
        hid1 = sb(pd, "hid1", [P, FJ, 2, MP], F16)
        x1b = sb(pd, "x1b", [P, 2, D], F32)
        sb(pd, "unused", [P, 2 * KC * TOK * 2 // 4 - FJ * MP - 2 * D], F32)
        hid = (sb(pd, "hid0", [P, FJ, 2, MP], F16), hid1)
        ob = sb(pd, "ob", [P, 2, D], F32)
        pd.close()

        consts_ready = sem("consts_ready")
        gates_in = sem("gates_in"); tanh_ready = sem("tanh_ready")
        wq_in = [sem(f"wq_in{i}") for i in range(4)]
        wqhi_ready = sem("wqhi_ready"); wqlo_ready = sem("wqlo_ready")
        x_in = [sem(f"x_in{i}") for i in range(2)]
        mv_ready = sem("mv_ready"); vep_ready = sem("vep_ready")
        xrs_ready = sem("xrs_ready"); xn_ready = sem("xn_ready"); xT_ready = sem("xT_ready")
        xhi_ready = sem("xhi_ready"); xlo_ready = sem("xlo_ready")
        q_ready = sem("q_ready"); qsq_ready = sem("qsq_ready"); qss_ready = sem("qss_ready")
        qms_ready = sem("qms_ready"); qrs_ready = sem("qrs_ready"); qhat_ready = sem("qhat_ready")
        qhi_ready = sem("qhi_ready"); qlo_ready = sem("qlo_ready"); qT_ready = sem("qT_ready")
        qTa_ready = sem("qTa_ready"); qTb_ready = sem("qTb_ready")
        q_saved = [sem(f"q_saved{i}") for i in range(2)]

        wk_in = sem("wk_in"); wkhi_ready = sem("wkhi_ready"); wklo_ready = sem("wklo_ready")
        ctx_in = [sem(f"ctx_in{i}") for i in range(3)]
        q_in = [sem(f"q_in{i}") for i in range(2)]
        gw_in = [sem(f"gw_in{i}") for i in range(2)]
        chi_ready = sem("chi_ready"); clo_ready = sem("clo_ready"); kv_ready = sem("kv_ready")
        ksq_ready = sem("ksq_ready"); kss_ready = sem("kss_ready"); kms_ready = sem("kms_ready")
        krs_ready = sem("krs_ready"); khat_ready = sem("khat_ready"); khi_ready = sem("khi_ready")
        klo_ready = sem("klo_ready"); kT_ready = sem("kT_ready"); kst_ready = sem("kst_ready")
        v1_ready = sem("v1_ready"); vres_ready = sem("vres_ready"); v2_ready = sem("v2_ready")
        v3_ready = sem("v3_ready")
        s_ready = sem("s_ready"); p_ready = sem("p_ready"); phi_ready = sem("phi_ready")
        plo_ready = sem("plo_ready"); pv_done = sem("pv_done"); o_ready = sem("o_ready")
        pool_step = sem("pool_step"); att_ready = sem("att_ready")
        att_saved = [sem(f"att_saved{i}") for i in range(2)]
        gsum_ready = sem("gsum_ready"); gmat_ready = sem("gmat_ready")
        gall_ready = sem("gall_ready"); thr_step = sem("thr_step")

        lx_in = [sem(f"lx_in{i}") for i in range(4)]
        x1_ready = sem("x1_ready"); ln_saved = [sem(f"ln_saved{i}") for i in range(4)]
        stage_in = [sem(f"stage_in{i}") for i in range(4)]
        lmv_ready = sem("lmv_ready"); lve_ready = sem("lve_ready")
        lrs_ready = sem("lrs_ready"); cn_ready = sem("cn_ready"); cnh_ready = sem("cnh_ready")
        cnl_ready = sem("cnl_ready"); cnT_ready = sem("cnT_ready")
        xnTh_ready = sem("xnTh_ready"); xnTl_ready = sem("xnTl_ready")
        w_in = [sem(f"w_in{i}") for i in range(2)]
        wneg_ready = sem("wneg_ready"); wquant_ready = sem("wquant_ready")
        h_ready = sem("h_ready"); sg_ready = sem("sg_ready"); hf_ready = sem("hf_ready")
        hh_ready = sem("hh_ready"); hl_ready = sem("hl_ready")
        hid_saved = [sem(f"hid_saved{i}") for i in range(2)]
        hid_in = [sem(f"hid_in{i}") for i in range(2)]
        x1_in = [sem(f"x1_in{i}") for i in range(2)]
        y_ready = sem("y_ready"); ob_ready = sem("ob_ready")
        out_saved = [sem(f"out_saved{i}") for i in range(2)]

        def tiles_of_x(eng, step):
            for i in range(2):
                step(i, i, False)
            with eng.Fori(1, NT // 2 - 1) as pair:
                for s in range(2):
                    step(pair * 2 + s, s, False)
            for i in (NT - 2, NT - 1):
                step(i, i % 2, i)

        def units(eng, unit, group=None):
            if group:
                group(0)
            for u in range(4):
                unit(u, u % 2, min(u, 2), u, 0, False)
            with eng.Fori(2, B // 2) as pair:
                for s in range(2):
                    unit(pair * 2 + s, s, 2, pair * 2 + s, 0, False)
            with eng.Fori(1, G - 1) as g:
                if group:
                    group(g)
                with eng.Fori(0, B // 2) as pair:
                    for s in range(2):
                        unit(g * B + pair * 2 + s, s, 2, pair * 2 + s, g, False)
            if group:
                group(G - 1)
            for b in range(B):
                unit((G - 1) * B + b, b % 2, 2, b, G - 1, b >= LNLAG)
            unit(U, 0, U, None, None, False)
            unit(U + 1, 1, U + 1, None, None, False)

        def projects(k):
            return k < U

        def attends(k, r, lag):
            return (k >= 2 or (k == 1 and r >= lag)) and k <= U or (k == U + 1 and r < lag)

        def behind(k, t, n):
            if k == 0:
                return t >= n
            return k < U or (k == U and t < n)

        LN_FIRST = {10: 2, 11: 4, 12: 7, 13: 8}
        LN_SLOT = {10: 2, 11: 3, 12: 1, 13: 0, 14: 2, 15: 3}

        def ln_tiles(u, k, t, ln, stage):
            after = {"add": 0, "stats": 1, "norm": 2, "low": 2 if ln else 3}[stage]
            if ln:
                i = 2 * (u - (G - 1) * B - LNLAG)
                return [i + h for h in range(2) if t - 3 * h == after]
            return [i for i, n in LN_FIRST.items() if k >= U and n == (k - U) * KT + t - after]

        def ln_slot(i):
            return LN_SLOT.get(i, 0)

        def ln_uses(i):
            return sum(ln_slot(n) == ln_slot(i) for n in range(i))

        X_TRANSPOSED = ((0, 1, 2, 3, 4), (5, 6, 7), (8, 9, 10), (11, 12), (13,), (14, 15), (), ())
        X_OUT = (range(0, 11), range(11, 13), range(13, 16), ())

        def phase_a_over(eng):
            eng.wait_ge(qTa_ready, 2 * NT)
            eng.wait_ge(qTb_ready, 2 * NT)

        def phase_b_over(eng):
            eng.wait_ge(pv_done, NQ * U)
            eng.wait_ge(o_ready, 8 * U)
            eng.wait_ge(gall_ready, 1)

        block = top.enter_context(nc.Block())

        @block.sync
        def _(sp):
            sp.dma_start(gates[:, :], gates_d).then_inc(gates_in, 16)
            for i in range(2):
                sp.dma_start(xraw[:, i, :], x_d[i, :, :]).then_inc(x_in[i], 16)
            for kc in range(KC):
                if kc >= 4:
                    sp.wait_ge(wqlo_ready, kc - 3)
                sp.dma_start(wqraw[:, kc % 4, :], wq_d[:, kc, :]).then_inc(wq_in[kc % 4], 16)
            sp.dma_start(wkraw[:, :, :], wkv_d[0, :, :, :]).then_inc(wk_in, 16)

            def save_q(h, i, c):
                sp.wait_ge(qTa_ready, h + 1)
                sp.wait_ge(qTb_ready, h + 1)
                for g in range(2):
                    sp.dma_start(qst_d[2 * c + g, :, :, bass.ds(i * P, P)],
                                 qTs[:, c, HG * g:HG * g + HG, :]).then_inc(q_saved[c], 16)

            def step_a(i, par, last):
                if not last:
                    sp.wait_ge(xn_ready, i + 1)
                    sp.dma_start(xraw[:, par, :], x_d[i + 2, :, :]).then_inc(x_in[par], 16)
                if not (isinstance(i, int) and i == 0):
                    save_q(2 * i - 2, i - 1, 0)
                    save_q(2 * i - 1, i - 1, 1)

            def load_ctx(T, slot, idx):
                wait(sp, clo_ready, T - 2)
                sp.dma_start(craw[:, slot, :, :], ctx_d[idx, :, :, :]).then_inc(ctx_in[slot], 16)

            tiles_of_x(sp, step_a)
            sp.wait_ge(wqlo_ready, KC)
            for t in range(3):
                load_ctx(t, t, t)
            for c in range(2):
                save_q(2 * NT - 2 + c, NT - 1, c)
            for c in range(2):
                sp.wait_ge(q_saved[c], 32 * NT)

            def save_att(a, par, qts=(0, 1)):
                sp.wait_ge(att_ready, 2 * a + 1 + qts[-1])
                for qt in qts:
                    n = QROWS[qt]
                    sp.dma_start(att_d[a, qt * P:qt * P + n, :],
                                 oatt[0:n, par, qt, :, :].rearrange("p h d -> p (h d)")
                                 ).then_inc(att_saved[par], 16)

            def load_w(j, s):
                for m in range(3):
                    sp.dma_start(wraw[:, 1 - s, m, :], wffn_d[m * (FJ // 2) + j, :, s, :]).then_inc(w_in[s], 16)

            def ln_load(i):
                s, b = ln_slot(i), i // 2
                if ln_slot(i) == 0:
                    sp.wait_ge(wklo_ready, KC * G)
                else:
                    sp.wait_ge(kv_ready, KT * U)
                sp.wait_ge(att_saved[b % 2], 32 * (((G - 1) * B + b) // 2 + 1) - (16 if i == NL - 2 else 0))
                wait(sp, ln_saved[s], 32 * ln_uses(i))
                cx, ca, _ = ln_mem[s]
                sp.dma_start(cx[:, :], x_d.rearrange("i p d -> (i p) d")[i * LT:i * LT + LT, :]
                             ).then_inc(lx_in[s], 16)
                for g in range(G):
                    r0 = LT * (i % 2)
                    sp.dma_start(ca[:, GC * g:GC * g + GC], att_d[g * B + b, r0:r0 + LT, :]).then_inc(lx_in[s], 16)

            def ln_save(i):
                s = ln_slot(i)
                _, ca, cn = ln_mem[s]
                sp.wait_ge(cnl_ready, i + 1)
                sp.dma_start(x1_d[i * LT:i * LT + LT, :], ca[:, :]).then_inc(ln_saved[s], 16)
                sp.dma_start(cn_d[i * LT:i * LT + LT, :, :], cn[:, :, :]).then_inc(ln_saved[s], 16)

            def unit_b(u, par, k, b, g, ln):
                if projects(k):
                    for t in range(KT):
                        if k or t >= 3:
                            load_ctx(u * KT + t, (par * KT + t) % 3, b * KT + t)
                        if t == KT - 1:
                            if k >= 2:
                                sp.wait_ge(s_ready, (u - 1) * NQ)
                            sp.dma_start(qT[:, par, :, :],
                                         qst_d[g, :, :, bass.ds(b * S, S)]).then_inc(q_in[par], 16)
                        if t == 1 and k >= 2 and not (isinstance(u, int) and u == 2):
                            save_att(u - 3, 1 - par)
                        if ln and t in (1, 4):
                            i = 2 * (b - LNLAG) + t // 4
                            if i:
                                ln_save(i - 1)
                            ln_load(i)
                        if t == 2:
                            if k >= 2:
                                sp.wait_ge(gsum_ready, u * 2 - 2)
                            sp.dma_start(gbuf[:, par, :, :], wffn_d[u, :, :, :]).then_inc(gw_in[par], 16)
                if k == U:
                    load_ctx(U * KT, 0, 0)
                    sp.wait_ge(gsum_ready, 2 * U - 2)
                    sp.dma_start(gbuf[:, 0, :, :], wffn_d[U, :, :, :]).then_inc(gw_in[0], 16)
                if k == U:
                    save_att(U - 3, 1)
                    for i in (10, 11):
                        ln_load(i)
                    ln_save(9)
                    save_att(U - 2, 0)
                    for i in (12, 13):
                        ln_load(i)
                    sp.wait_ge(gsum_ready, 2 * WPAIRS)
                    sp.wait_ge(kst_ready, KT * U)
                    load_w(0, 0)
                    ln_save(10)
                    ln_save(11)

            def prefetch_w(g):
                sp.wait_ge(wklo_ready, KC * g)
                sp.dma_start(wkraw[:, :, :], wkv_d[g, :, :, :]).then_inc(wk_in, 16)

            unit_b(0, 0, 0, 0, 0, False)
            prefetch_w(1)
            for u in range(1, 4):
                unit_b(u, u % 2, min(u, 2), u, 0, False)
            with sp.Fori(2, B // 2) as pair:
                for s in range(2):
                    unit_b(pair * 2 + s, s, 2, pair * 2 + s, 0, False)
            with sp.Fori(1, G - 1) as g:
                for s in range(2):
                    unit_b(g * B + s, s, 2, s, g, False)
                prefetch_w(g + 1)
                with sp.Fori(1, B // 2) as pair:
                    for s in range(2):
                        unit_b(g * B + pair * 2 + s, s, 2, pair * 2 + s, g, False)
            for b in range(B):
                unit_b((G - 1) * B + b, b % 2, 2, b, G - 1, b >= LNLAG)
            unit_b(U, 0, U, None, None, False)
            unit_b(U + 1, 1, U + 1, None, None, False)

            phase_b_over(sp)

            def load_stage(i):
                s = ln_slot(i)
                sp.wait_ge(ln_saved[s], 32 * (ln_uses(i) + 1))
                wait(sp, cnT_ready, i - 3)
                sp.dma_start(stage[:, i % 4, :, :], cn_d[i * LT:i * LT + LT, :, :]).then_inc(stage_in[i % 4], 16)

            for i in range(4):
                load_stage(i)
            load_stage(4)
            save_att(U - 1, 1, (0,))
            ln_load(NL - 2)
            load_stage(5)
            load_stage(6)
            save_att(U - 1, 1, (1,))
            ln_load(NL - 1)
            load_stage(7)
            load_stage(8)
            ln_save(12)
            ln_save(13)
            for i in range(9, 12):
                load_stage(i)
            load_w(0, 1)
            ln_save(14)
            ln_save(15)
            for i in range(12, NL):
                load_stage(i)

            def load_hid(m, par):
                sp.dma_start(hid[par][:, :, :, :], hid_d[:, :, :, bass.ds(m * MP, MP)]).then_inc(hid_in[par], 16)

            def save_hid(j, s, last=False):
                for c, (c0, n) in enumerate(CH):
                    if last and c == 1:
                        sp.wait_ge(hid_saved[0], 32 * FJ - 16)
                        sp.wait_ge(wquant_ready, 3 * FJ)
                        sp.wait_ge(h_ready, 4 * (FJ - 1))
                        load_hid(0, 0)
                    sp.wait_ge(hl_ready, j * 4 + (c + 1))
                    sp.dma_start(hid_d[:, j, :, c0:c0 + n], hh[:, c % 2, :, 0:n]).then_inc(hid_saved[c % 2], 16)

            with sp.Fori(1, FJ // 2) as pair:
                for s in range(2):
                    sp.wait_ge(wquant_ready, pair * 6 + (3 * s - 3))
                    load_w(pair, s)
                    save_hid(pair * 2 + (s - 2), s)
            for s in range(2):
                save_hid(FJ - 2 + s, s, s == 1)
            for s in range(2):
                sp.wait_ge(hid_saved[s], 32 * FJ)

            def load_x1(m, tt):
                sp.dma_start(x1b[:, tt, :], x1_d[bass.ds(m * MP + tt * P, P), :]).then_inc(x1_in[tt], 16)

            def save_out(m, tt):
                sp.wait_ge(ob_ready, m * 2 + tt + 1)
                sp.dma_start(out_d[bass.ds(m * MP + tt * P, P), :], ob[:, tt, :]).then_inc(out_saved[tt], 16)

            load_hid(1, 1)
            for tt in range(2):
                load_x1(0, tt)

            def step_d(m, par, more_x1, more_hid):
                if more_hid:
                    sp.wait_ge(y_ready, m * 2 + 2)
                    load_hid(m + 2, par)
                for tt in range(2):
                    save_out(m, tt)
                    if more_x1:
                        load_x1(m + 1, tt)

            step_d(0, 0, True, True)
            with sp.Fori(0, 2) as pair:
                for s in range(2):
                    step_d(pair * 2 + (s + 1), 1 - s, True, True)
            step_d(NM - 2, 1, True, False)
            step_d(NM - 1, 0, False, False)
            for tt in range(2):
                sp.wait_ge(out_saved[tt], 16 * NM)

        @block.gpsimd
        def _(pool):
            pool.memset(ident[:, :], 0.0).then_inc(pool_step, 1)
            pool.memset(identh[:, :], 0.0).then_inc(pool_step, 1)
            pool.memset(ones[:, :], 1.0).then_inc(consts_ready, 1)
            pool.memset(mhalf[:, :], -0.5).then_inc(consts_ready, 1)
            pool.memset(mone[:, :], -1.0).then_inc(consts_ready, 1)
            pool.memset(lneps[:, :], LN_EPS).then_inc(consts_ready, 1)
            pool.memset(rmseps[:, :], DH * RMS_EPS).then_inc(consts_ready, 1)
            pool.wait_ge(pool_step, 2)
            for m in (ident, identh):
                pool.affine_select(out=m[:, :], in_=m[:, :], compare_op=ALU.not_equal, fill=1.0, base=0,
                                   pattern=[[-1, P]], channel_multiplier=1).then_inc(consts_ready, 1)
            pool.wait_ge(consts_ready, 7)

            def x_rstd(i, par):
                pool.wait_ge(mv_ready, i + 1)
                wait(pool, xrs_ready, i)
                pool.tensor_tensor(vep[:, :], bag[:, par, 1:2], lneps[:, :], ALU.add).then_inc(vep_ready, 1)
                pool.wait_ge(vep_ready, i + 1)
                wait(pool, xn_ready, i - 1)
                pool.tensor_tensor(xrs[:, par, :], vep[:, :], mhalf[:, 0:1], ALU.pow).then_inc(xrs_ready, 1)

            def q_rstd(h):
                pool.wait_ge(qss_ready, h + 1)
                wait(pool, qrs_ready, h)
                pool.tensor_tensor(qms[:, :], qss[:, :], rmseps[:, :], ALU.add).then_inc(qms_ready, 1)
                pool.wait_ge(qms_ready, h + 1)
                wait(pool, qhat_ready, h)
                pool.tensor_tensor(qrs[:, :], qms[:, :], mhalf[:, :], ALU.pow).then_inc(qrs_ready, 1)

            x_rstd(0, 0)
            x_rstd(1, 1)

            def step_a(i, par, last):
                q_rstd(2 * i)
                q_rstd(2 * i + 1)
                if not last:
                    x_rstd(i + 2, par)

            tiles_of_x(pool, step_a)

            phase_a_over(pool)

            def k_rstd(T):
                pool.wait_ge(kss_ready, T + 1)
                wait(pool, krs_ready, T)
                pool.tensor_tensor(kms[0:KW, :], kss[0:KW, :], rmseps[0:KW, 0:HG], ALU.add
                                   ).then_inc(kms_ready, 1)
                pool.wait_ge(kms_ready, T + 1)
                wait(pool, khat_ready, T)
                pool.tensor_tensor(krs[0:KW, :], kms[0:KW, :], mhalf[0:KW, 0:HG], ALU.pow
                                   ).then_inc(krs_ready, 1)

            o_step = sem("o_step")

            def attend_out(a, par, qt):
                n = QROWS[qt]
                o = oraw[0:n, par, qt, :, :]
                done = a * 8 + 4 * qt
                if qt == 0:
                    pool.wait_ge(o_ready, a * 8 + 8)
                    wait(pool, att_saved[par], (a - par) * 16)
                wait(pool, att_ready, a * 2 + qt)
                pool.tensor_tensor(osum[0:n, :, :], o[:, :, 0:DH], o[:, :, 2 * DH:3 * DH], ALU.add
                                   ).then_inc(o_step, 1)
                pool.wait_ge(o_step, done + 1)
                pool.tensor_tensor(osum[0:n, :, :], osum[0:n, :, :], o[:, :, DH:2 * DH], ALU.add
                                   ).then_inc(o_step, 1)
                pool.tensor_tensor(oinv[0:n, :], o[:, :, 3 * DH], mone[0:n, :], ALU.pow).then_inc(o_step, 1)
                pool.wait_ge(o_step, done + 3)
                pool.tensor_tensor(oinv[0:n, :], oinv[0:n, :], tanhs[0:n, 0:1].to_broadcast([n, HG]), ALU.mult
                                   ).then_inc(o_step, 1)
                pool.wait_ge(o_step, done + 4)
                pool.tensor_tensor(oatt[0:n, par, qt, :, :], osum[0:n, :, :],
                                   oinv[0:n, :].unsqueeze(2).to_broadcast([n, HG, DH]), ALU.mult
                                   ).then_inc(att_ready, 1)

            def ln_add(i):
                s = ln_slot(i)
                cx, ca, _ = ln_mem[s]
                pool.wait_ge(lx_in[s], 80 * (ln_uses(i) + 1))
                pool.tensor_tensor(ca[:, :], ca[:, :], cx[:, :], ALU.add).then_inc(x1_ready, 1)

            def ln_rstd(i):
                s = ln_slot(i)
                pool.wait_ge(lmv_ready, i + 1)
                wait(pool, lrs_ready, i)
                pool.tensor_tensor(cve[:, :], cag[:, s, 1:2], lneps[0:LT, :], ALU.add).then_inc(lve_ready, 1)
                pool.wait_ge(lve_ready, i + 1)
                pool.tensor_tensor(crs[:, s, :], cve[:, :], mhalf[0:LT, 0:1], ALU.pow).then_inc(lrs_ready, 1)

            def ln_low(i):
                cx, _, cn = ln_mem[ln_slot(i)]
                pool.wait_ge(cnh_ready, i + 1)
                pool.tensor_tensor(cn[:, 1, :], cx[:, :], cn[:, 0, :], ALU.subtract).then_inc(cnl_ready, 1)

            def unit_b(u, par, k, b, g, ln):
                for t in range(KT):
                    if behind(k, t, 1):
                        k_rstd(u * KT + (t - 1))
                    if k >= 2 and t in (3, 4):
                        attend_out(u - 2, par, t - 3)
                    for i in ln_tiles(u, k, t, ln, "low"):
                        ln_low(i)
                    for i in ln_tiles(u, k, t, ln, "add"):
                        ln_add(i)
                    for i in ln_tiles(u, k, t, ln, "stats"):
                        ln_rstd(i)

            pool.wait_ge(tanh_ready, 1)
            units(pool, unit_b)
            ln_add(14)
            ln_rstd(14)
            ln_add(15)
            ln_low(14)
            ln_rstd(15)
            ln_low(15)

        @block.scalar
        def _(act):
            act.wait_ge(gates_in, 16)
            act.activation(tanhs[:, :], gates[:, :], ACT.Tanh).then_inc(tanh_ready, 1)

            def x_high(i, par):
                act.wait_ge(xT_ready, i + 1)
                wait(act, q_ready, 2 * (i - 1))
                act.activation(xhi[:, par, :], ps[:, 0:2, :].rearrange("p b n -> p (b n)"), ACT.Copy
                               ).then_inc(xhi_ready, 1)

            x_high(0, 0)
            for kc in range(KC):
                act.wait_ge(wq_in[kc % 4], 16 * (kc // 4 + 1))
                act.activation(wqhi[:, kc, :], wqraw[:, kc % 4, :], ACT.Copy).then_inc(wqhi_ready, 1)

            def w_high(g, kcs=range(KC)):
                act.wait_ge(wk_in, g * 16 + 16)
                if not isinstance(g, int):
                    act.wait_ge(kv_ready, g * (B * KT))
                for kc in kcs:
                    act.activation(wkhi[:, kc, :], wkraw[:, kc, :], ACT.Copy).then_inc(wkhi_ready, 1)

            def half(h, c):
                b = 2 + c
                act.wait_ge(q_ready, h + 1)
                wait(act, qss_ready, h)
                act.activation(qsq[:, :, :], bank(b).rearrange("p (h d) -> p h d", d=DH), ACT.Square
                               ).then_inc(qsq_ready, 1)

            def half_high(h, c):
                act.wait_ge(qhat_ready, h + 1)
                wait(act, qT_ready, h - 1)
                act.activation(qnat[:, c, :, 0:4:2, :],
                               qhat[:, :, :].unsqueeze(2).to_broadcast([P, 16, 2, DH]), ACT.Copy
                               ).then_inc(qhi_ready, 1)

            def half_out(h, i, c):
                act.wait_ge(qT_ready, h + 1)
                if not isinstance(i, int) or i > 0:
                    act.wait_ge(q_saved[c], i * 32)
                act.activation(qTs[:, c, 0:8, :], bank(4 + 2 * c, F16).rearrange("p (h n) -> p h n", n=P),
                               ACT.Copy).then_inc(qTa_ready, 1)

            def step_a(i, par, last):
                first = isinstance(i, int) and i == 0
                for c in range(2):
                    h = 2 * i + c
                    half(h, c)
                    if not first:
                        half_out(h - 2, i - 1, c)
                    if c == 0 and (not last or last == NT - 2):
                        x_high(i + 1, 1 - par)
                    if last:
                        n = 2 * (h - 2 * (NT - 2))
                        w_high(0, range(n, n + 2))
                    half_high(h, c)

            tiles_of_x(act, step_a)
            for c in range(2):
                half_out(2 * NT - 2 + c, NT - 1, c)

            phase_a_over(act)

            def ln_high(i):
                cx, _, cn = ln_mem[ln_slot(i)]
                act.wait_ge(cn_ready, i + 1)
                act.activation(cn[:, 0, :], cx[:, :], ACT.Copy).then_inc(cnh_ready, 1)

            def ctx_high(T, par, slot, use):
                act.wait_ge(ctx_in[slot], use)
                wait(act, kv_ready, T - 1)
                act.activation(chi[:, par, :, :], craw[:, slot, :, :], ACT.Copy).then_inc(chi_ready, 1)

            ctx_high(0, 0, 0, 16)

            def group_b(g):
                if not (isinstance(g, int) and g == 0):
                    w_high(g)

            def unit_b(u, par, k, b, g, ln):
                for r in range(NQ):
                    t, j = r // 4, r % 4
                    Tb = u * KT + (t - 1)
                    pt = (par * KT + t - 1) % 2
                    vt = (t - 1) % KT
                    vp = par if t >= 1 else 1 - par

                    def value_high():
                        wait(act, pv_done, (u - 1) * NQ - 2 if t == 1 else (u - 1) * NQ if t > 1
                             else (u - 2) * NQ)
                        act.activation(val[0:KW, vp, vt, :, DH:2 * DH],
                                       bank(pt)[0:KW, GC:2 * GC].rearrange("p (h d) -> p h d", d=DH),
                                       ACT.Copy).then_inc(v1_ready, 1)

                    if j == 0 and behind(k, t, 1):
                        act.wait_ge(kv_ready, Tb + 1)
                        wait(act, kss_ready, Tb)
                        act.activation(ksq[0:KW, :, :],
                                       bank(pt)[0:KW, 0:GC].rearrange("p (h d) -> p h d", d=DH), ACT.Square
                                       ).then_inc(ksq_ready, 1)
                        if t != 1:
                            value_high()
                    if j == 1 and projects(k):
                        tn = par * KT + t + 1
                        slot = tn % 3
                        uses = (u - par) * 32 + 16 * (tn // 3 + 1)
                        ctx_high(u * KT + (t + 1), tn % 2, slot, uses)
                    if j == 3 and behind(k, t, 1):
                        act.wait_ge(vres_ready, Tb + 1)
                        act.activation(val[0:KW, vp, vt, :, 2 * DH:3 * DH], vres[0:KW, :, :], ACT.Copy
                                       ).then_inc(v2_ready, 1)
                        act.wait_ge(khat_ready, Tb + 1)
                        wait(act, kT_ready, Tb - 1)
                        act.activation(knat[0:KW, pt, :, 0:2, :],
                                       khat[0:KW, :, :].unsqueeze(2).to_broadcast([KW, HG, 2, DH]),
                                       ACT.Copy).then_inc(khi_ready, 1)
                    if r % 6 == 2 and attends(k, r, 14):
                        w = (r - 14) // 6
                        pr, op = (w % 4), (par if w < 0 else 1 - par)
                        act.wait_ge(pv_done, (u - 1) * NQ + 6 * w + 6)
                        if w == 0:
                            wait(act, att_ready, (u - 2) * 2)
                        for qt, n in enumerate(QROWS):
                            c0 = 2 * VW * qt
                            act.activation(oraw[0:n, op, qt, 2 * pr:2 * pr + 2, :],
                                           bank(6 + pr % 2)[0:n, c0:c0 + 2 * VW].rearrange(
                                               "p (h d) -> p h d", d=VW), ACT.Copy).then_inc(o_ready, 1)
                    if attends(k, r, SHIFT + 1):
                        e = r - SHIFT - 1
                        R = (u - 1) * NQ + e
                        act.wait_ge(p_ready, R + 1)
                        if not (k == 1 and e < 6):
                            act.wait_ge(pv_done, R - 5)
                        act.activation(phi[0:KW, e % 6, :, :],
                                       pf[0:KW, e % 6, :].rearrange("p (t n) -> p t n", t=2), ACT.Copy
                                       ).then_inc(phi_ready, 1)
                    if attends(k, r, SHIFT):
                        e = r - SHIFT
                        R = (u - 1) * NQ + e
                        act.wait_ge(s_ready, R + 1)
                        if not (k == 1 and e < 6):
                            act.wait_ge(plo_ready, R - 5)
                        act.activation(pf[0:KW, e % 6, :], bank(3 + e % 3)[0:KW, 0:2 * S], ACT.Exp,
                                       bias=LN128, scale=SCALE).then_inc(p_ready, 1)
                    if j == 1 and t == 1 and behind(k, t, 1):
                        value_high()
                    if j == (1 if ln else 3):
                        for i in ln_tiles(u, k, t, ln, "norm"):
                            ln_high(i)

            units(act, unit_b, group_b)

            phase_b_over(act)

            def x_out(i):
                act.wait_ge(cnT_ready, i + 1)
                act.activation(xnTh[:, :, i * LT:i * LT + LT],
                               bank(4 + 2 * (i % 2), F16).rearrange("p (k n) -> p k n", n=P)[:, :, 0:LT],
                               ACT.Copy).then_inc(xnTh_ready, 1)

            def hidden(j, first):
                for c, (c0, n) in enumerate(CH):
                    m = j * 4 + c
                    if first:
                        for i in X_OUT[c]:
                            x_out(i)
                            if i in (4, 7):
                                ln_high(14 if i == 4 else 15)
                    act.wait_ge(h_ready, m + 1)
                    wait(act, hf_ready, m - 1)
                    act.activation(sg[:, c % 2, 0:n], bank(c % 2)[:, 0:n], ACT.Sigmoid).then_inc(sg_ready, 1)
                    act.wait_ge(hf_ready, m + 1)
                    if not (first and c < 2):
                        act.wait_ge(hid_saved[c % 2], j * 32 + 16 * (c // 2))
                    act.activation(hh[:, c % 2, 0, 0:n], hf[:, c % 2, 0:n], ACT.Copy).then_inc(hh_ready, 1)

            hidden(0, True)
            with act.Fori(1, FJ) as j:
                hidden(j, False)

        @block.vector
        def _(dve):
            def x_norm(i, par):
                dve.wait_ge(x_in[par], (i - par) * 8 + 16)
                wait(dve, mv_ready, i)
                wait(dve, xn_ready, i - 1)
                for c in range(2):
                    dve.bn_stats(bst[:, c, :], xraw[:, par, 512 * c:512 * c + 512])
                dve.drain()
                dve.bn_aggr(bag[:, par, :], bst[:, :, :]).then_inc(mv_ready, 1)

            def x_norm2(i, par):
                dve.wait_ge(xrs_ready, i + 1)
                wait(dve, xT_ready, i)
                dve.tensor_scalar(xn[:, :], xraw[:, par, :], bag[:, par, 0:1], xrs[:, par, :], ALU.subtract,
                                  ALU.mult).then_inc(xn_ready, 1)

            def x_low(i, par):
                dve.wait_ge(xhi_ready, i + 1)
                dve.tensor_tensor(xlo[:, par, :], ps[:, 0:2, :].rearrange("p b n -> p (b n)"),
                                  xhi[:, par, :].bitcast(F32), ALU.subtract).then_inc(xlo_ready, 1)

            x_norm(0, 0)
            x_norm(1, 1)
            x_norm2(0, 0)
            x_low(0, 0)
            for kc in range(KC):
                dve.wait_ge(wqhi_ready, kc + 1)
                dve.tensor_tensor(wqlo[:, kc, :], wqraw[:, kc % 4, :], wqhi[:, kc, :].bitcast(F32),
                                  ALU.subtract).then_inc(wqlo_ready, 1)
            x_norm2(1, 1)

            def w_low(g, kcs=range(KC)):
                for kc in kcs:
                    dve.wait_ge(wkhi_ready, g * KC + (kc + 1))
                    dve.tensor_tensor(wklo[:, kc, :], wkraw[:, kc, :], wkhi[:, kc, :].bitcast(F32),
                                      ALU.subtract).then_inc(wklo_ready, 1)

            def half_sums(h):
                dve.wait_ge(qsq_ready, h + 1)
                wait(dve, qrs_ready, h)
                dve.tensor_reduce(qss[:, :], qsq[:, :, :], AX_X, ALU.add).then_inc(qss_ready, 1)

            def half_norm(h, c):
                dve.wait_ge(qrs_ready, h + 1)
                wait(dve, qlo_ready, h)
                dve.scalar_tensor_tensor(out=qhat[:, :, :], in0=bank(2 + c).rearrange("p (h d) -> p h d", d=DH),
                                         scalar=ROOT, in1=qrs[:, :].unsqueeze(2).to_broadcast([P, 16, DH]),
                                         op0=ALU.mult, op1=ALU.mult).then_inc(qhat_ready, 1)

            def half_low(h, c):
                dve.wait_ge(qhi_ready, h + 1)
                dve.tensor_tensor(qnat[:, c, :, 1:4:2, :],
                                  qhat[:, :, :].unsqueeze(2).to_broadcast([P, 16, 2, DH]),
                                  qnat[:, c, :, 0:4:2, :], ALU.subtract).then_inc(qlo_ready, 1)

            def half_out(h, i, c):
                dve.wait_ge(qT_ready, h + 1)
                if not isinstance(i, int) or i > 0:
                    dve.wait_ge(q_saved[c], i * 32)
                dve.tensor_copy(qTs[:, c, 8:16, :], bank(5 + 2 * c, F16).rearrange("p (h n) -> p h n", n=P)
                                ).then_inc(qTb_ready, 1)

            def step_a(i, par, last):
                first = isinstance(i, int) and i == 0
                for c in range(2):
                    h = 2 * i + c
                    half_sums(h)
                    if not (first and c == 0):
                        half_low(h - 1, 1 - c)
                    if not first:
                        half_out(h - 2, i - 1, c)
                    if c == 0 and (not last or last == NT - 2):
                        x_low(i + 1, 1 - par)
                    if last:
                        n = 2 * (h - 2 * (NT - 2))
                        w_low(0, range(n, n + 2))
                    if c == 1 and not last:
                        x_norm(i + 2, par)
                    half_norm(h, c)
                if not last:
                    x_norm2(i + 2, par)

            tiles_of_x(dve, step_a)
            half_low(2 * NT - 1, 1)
            for c in range(2):
                half_out(2 * NT - 2 + c, NT - 1, c)

            phase_a_over(dve)
            dve.memset(val[:, :, :, :, 3 * DH:VW], 1.0).then_inc(v3_ready, 1)

            def ln_stats(i):
                s = ln_slot(i)
                ca = ln_mem[s][1]
                dve.wait_ge(x1_ready, i + 1)
                wait(dve, lmv_ready, i)
                for c in range(2):
                    dve.bn_stats(cst[:, c, :], ca[:, 512 * c:512 * c + 512])
                dve.drain()
                dve.bn_aggr(cag[:, s, :], cst[:, :, :]).then_inc(lmv_ready, 1)

            def ln_norm(i):
                s = ln_slot(i)
                cx, ca, _ = ln_mem[s]
                dve.wait_ge(lrs_ready, i + 1)
                dve.tensor_scalar(cx[:, :], ca[:, :], cag[:, s, 0:1], crs[:, s, :], ALU.subtract, ALU.mult
                                  ).then_inc(cn_ready, 1)

            def ctx_low(T, par, slot):
                dve.wait_ge(chi_ready, T + 1)
                dve.tensor_tensor(clo[:, par, :, :], craw[:, slot, :, :], chi[:, par, :, :].bitcast(F32),
                                  ALU.subtract).then_inc(clo_ready, 1)

            ctx_low(0, 0, 0)

            def group_b(g):
                if not (isinstance(g, int) and g == 0):
                    w_low(g)

            def quantise(j, pair, s, ms=range(3)):
                dve.wait_ge(w_in[s], pair * 48 + 48)
                for m in ms:
                    n = j * 3 + m
                    wait(dve, wquant_ready, n)
                    dve.tensor_scalar(wneg[:, :], wraw[:, 1 - s, m, :], thr[:, 2, m:m + 1], None, ALU.is_lt
                                      ).then_inc(wneg_ready, 1)
                    dve.wait_ge(wneg_ready, n + 1)
                    if m < 2:
                        if m == 0:
                            wait(dve, h_ready, (j - 1) * 4)
                        dst = w12q[:, s, m, :, :].rearrange("p k n -> p (k n)")
                    else:
                        if isinstance(j, int) and j == 0:
                            for n in (12, 13):
                                dve.wait_ge(ln_saved[ln_slot(n)], 32 * (ln_uses(n) + 1))
                        dst = w3q[:, j, :]
                    dve.scalar_tensor_tensor(out=dst, in0=wraw[:, 1 - s, m, :], scalar=thr[:, 1, m:m + 1],
                                             in1=wneg[:, :], op0=ALU.is_gt, op1=ALU.subtract
                                             ).then_inc(wquant_ready, 1)

            def weight_sums():
                dve.wait_ge(gsum_ready, 2 * WPAIRS)
                dve.tensor_reduce(gmat[:, :], gsum[:, :].rearrange("p (m n) -> p m n", m=3), AX_X, ALU.add
                                  ).then_inc(gmat_ready, 1)

            def thresholds():
                dve.wait_ge(gall_ready, 1)
                dve.tensor_scalar(thr[:, 0, :], bank(0)[:, 0:3], 1.0 / (F * D), Q_EPS, ALU.mult, ALU.add
                                  ).then_inc(thr_step, 1)
                dve.wait_ge(thr_step, 1)
                dve.tensor_scalar(thr[:, 1, :], thr[:, 0, :], 0.5, None, ALU.mult).then_inc(thr_step, 1)
                dve.tensor_scalar(thr[:, 2, :], thr[:, 0, :], -0.5, None, ALU.mult).then_inc(thr_step, 1)
                dve.wait_ge(thr_step, 3)

            def unit_b(u, par, k, b, g, ln):
                for r in range(NQ):
                    t, j = r // 4, r % 4
                    Tb = u * KT + (t - 1)
                    pt = (par * KT + t - 1) % 2
                    vt = (t - 1) % KT
                    vp = par if t >= 1 else 1 - par
                    if k == U and r == 20:
                        weight_sums()
                    if k == U + 1 and r == 4:
                        thresholds()
                    if k == U + 1 and r == 6:
                        quantise(0, 0, 0, (0, 1))
                    if j == 0 and behind(k, t, 2):
                        dve.wait_ge(khi_ready, Tb)
                        dve.tensor_tensor(knat[0:KW, 1 - pt, :, 2:4, :],
                                          khat[0:KW, :, :].unsqueeze(2).to_broadcast([KW, HG, 2, DH]),
                                          knat[0:KW, 1 - pt, :, 0:2, :], ALU.subtract).then_inc(klo_ready, 1)
                    if j == 0 and behind(k, t, 1):
                        dve.wait_ge(ksq_ready, Tb + 1)
                        wait(dve, krs_ready, Tb)
                        dve.tensor_reduce(kss[0:KW, :], ksq[0:KW, :, :], AX_X, ALU.add).then_inc(kss_ready, 1)
                    if j == (2 if t == 1 else 1) and behind(k, t, 1):
                        dve.wait_ge(v1_ready, Tb + 1)
                        if k or t > 1:
                            dve.wait_ge(v3_ready, Tb + 1)
                        dve.tensor_tensor(vres[0:KW, :, :],
                                          bank(pt)[0:KW, GC:2 * GC].rearrange("p (h d) -> p h d", d=DH),
                                          val[0:KW, vp, vt, :, DH:2 * DH], ALU.subtract
                                          ).then_inc(vres_ready, 1)
                    if j == 1 and projects(k):
                        tn = par * KT + t + 1
                        ctx_low(u * KT + (t + 1), tn % 2, tn % 3)
                    if j == 2 and behind(k, t, 1):
                        dve.wait_ge(krs_ready, Tb + 1)
                        wait(dve, klo_ready, Tb)
                        dve.scalar_tensor_tensor(
                            out=khat[0:KW, :, :], in0=bank(pt)[0:KW, 0:GC].rearrange("p (h d) -> p h d", d=DH),
                            scalar=ROOT, in1=krs[0:KW, :].unsqueeze(2).to_broadcast([KW, HG, DH]),
                            op0=ALU.mult, op1=ALU.mult).then_inc(khat_ready, 1)
                    if j == 2 and behind(k, t, 2):
                        tt = (t - 2) % KT
                        kp = par if t >= 2 else 1 - par
                        dve.wait_ge(kT_ready, Tb)
                        wait(dve, s_ready, (u - 1) * NQ if t >= 2 else (u - 2) * NQ)
                        dve.tensor_copy(kst[:, kp, :, tt * KW:tt * KW + KW],
                                        bank(2, F16).rearrange("p (h n) -> p h n", n=P)[:, :, 0:KW]
                                        ).then_inc(kst_ready, 1)
                    if j == 3 and behind(k, t, 1):
                        dve.wait_ge(v2_ready, Tb + 1)
                        dve.tensor_tensor(val[0:KW, vp, vt, :, 0:DH], vres[0:KW, :, :],
                                          val[0:KW, vp, vt, :, 2 * DH:3 * DH], ALU.subtract
                                          ).then_inc(v3_ready, 1)
                    if r in (7, 15) and k <= U:
                        a = r // 8
                        if a == 0:
                            dve.wait_ge(gw_in[par], (u - par) * 8 + 16)
                        dve.tensor_reduce(gsum[:, bass.ds(u * 2 + a, 1)], gbuf[:, par, a, :], AX_X, ALU.add,
                                          apply_absolute_value=True).then_inc(gsum_ready, 1)
                    if attends(k, r, SHIFT + 1):
                        e = r - SHIFT - 1
                        dve.wait_ge(phi_ready, (u - 1) * NQ + e + 1)
                        dve.tensor_tensor(plo[0:KW, e % 6, :, :],
                                          pf[0:KW, e % 6, :].rearrange("p (t n) -> p t n", t=2),
                                          phi[0:KW, e % 6, :, :], ALU.subtract).then_inc(plo_ready, 1)
                    if j == (0 if ln else 2):
                        for i in ln_tiles(u, k, t, ln, "stats"):
                            ln_stats(i)
                    if j == (0 if ln else 3):
                        for i in ln_tiles(u, k, t, ln, "norm"):
                            ln_norm(i)

            units(dve, unit_b, group_b)

            dve.wait_ge(tanh_ready, 1)

            phase_b_over(dve)

            def x_out(i):
                dve.wait_ge(cnT_ready, i + 1)
                dve.tensor_copy(xnTl[:, :, i * LT:i * LT + LT],
                                bank(5 + 2 * (i % 2), F16).rearrange("p (k n) -> p k n", n=P)[:, :, 0:LT]
                                ).then_inc(xnTl_ready, 1)

            def hidden(j, first):
                for c, (c0, n) in enumerate(CH):
                    m = j * 4 + c
                    if first and c:
                        for i in X_OUT[c]:
                            x_out(i)
                        quantise(1, 0, 1, (c - 1,))
                    dve.wait_ge(sg_ready, m + 1)
                    if not (first and c < 2):
                        dve.wait_ge(hl_ready, m - 1)
                    dve.tensor_tensor(hf[:, c % 2, 0:n], bank(2 + c % 2)[:, 0:n], sg[:, c % 2, 0:n], ALU.mult
                                      ).then_inc(hf_ready, 1)
                    dve.wait_ge(hh_ready, m + 1)
                    dve.tensor_tensor(hh[:, c % 2, 1, 0:n], hf[:, c % 2, 0:n], hh[:, c % 2, 0, 0:n],
                                      ALU.subtract).then_inc(hl_ready, 1)

            for i in range(5):
                x_out(i)
            ln_stats(14)
            ln_norm(14)
            for i in range(5, 8):
                x_out(i)
            ln_stats(15)
            ln_norm(15)
            for i in range(8, 11):
                x_out(i)
            quantise(0, 0, 0, (2,))
            hidden(0, True)
            with dve.Fori(1, FJ // 2) as pair:
                quantise(pair * 2, pair, 0)
                hidden(pair * 2 - 1, False)
                quantise(pair * 2 + 1, pair, 1)
                hidden(pair * 2, False)
            hidden(FJ - 1, False)

            def result(m, par, first):
                for tt in range(2):
                    dve.wait_ge(y_ready, m * 2 + tt + 1)
                    dve.wait_ge(x1_in[tt], m * 16 + 16)
                    if not first:
                        dve.wait_ge(out_saved[tt], m * 16)
                    b0 = 4 * par + 2 * tt
                    dve.scalar_tensor_tensor(out=ob[:, tt, :], in0=ps[:, b0:b0 + 2, :].rearrange("p b n -> p (b n)"),
                                             scalar=tanhs[:, 1:2], in1=x1b[:, tt, :], op0=ALU.mult,
                                             op1=ALU.add).then_inc(ob_ready, 1)

            result(0, 0, True)
            with dve.Fori(0, NM // 2) as pair:
                result(pair * 2 + 1, 1, False)
                result(pair * 2 + 2, 0, False)

        @block.tensor
        def _(pe):
            pe.wait_ge(consts_ready, 7)

            def x_transpose(i):
                pe.wait_ge(xn_ready, i + 1)
                wait(pe, xlo_ready, i)
                for kc in range(KC):
                    mm = pe.transpose(ps[:, kc // 4, (kc % 4) * P:(kc % 4) * P + P],
                                      xn[:, kc * P:kc * P + P], ident[:, :])
                mm.then_inc(xT_ready, 1)

            def q_half(h, i, par, c, first):
                pe.wait_ge(xlo_ready, i + 1)
                wait(pe, qhat_ready, h - 1)
                for kc in range(KC):
                    if first:
                        pe.wait_ge(wqlo_ready, kc + 1)
                    cols = slice(512 * c, 512 * c + 512)
                    for n, (a, w) in enumerate(((xhi, wqhi), (xhi, wqlo), (xlo, wqhi))):
                        mm = pe.matmul(bank(2 + c), a[:, par, kc * P:kc * P + P], w[:, kc, cols],
                                       start=(kc == 0 and n == 0), stop=(kc == KC - 1 and n == 2))
                mm.then_inc(q_ready, 1)

            def q_stack(h, c):
                pe.wait_ge(qlo_ready, h + 1)
                wait(pe, qTa_ready, h - 1)
                wait(pe, qTb_ready, h - 1)
                for n in range(16):
                    b = 4 + 2 * c + n // 8
                    mm = pe.transpose(bank(b, F16)[:, (n % 8) * P:(n % 8) * P + P],
                                      qnat[:, c, n, :, :].rearrange("p a d -> p (a d)"), identh[:, :])
                mm.then_inc(qT_ready, 1)

            x_transpose(0)

            def step_a(i, par, last):
                first = isinstance(i, int) and i == 0
                for c in range(2):
                    q_half(2 * i + c, i, par, c, first and c == 0)
                    if not first:
                        q_stack(2 * i - 2 + c, c)
                    if c == 0 and (not last or last == NT - 2):
                        x_transpose(i + 1)

            tiles_of_x(pe, step_a)
            for c in range(2):
                q_stack(2 * NT - 2 + c, c)

            phase_a_over(pe)
            pe.wait_ge(v3_ready, 1)

            def unit_b(u, par, k, b, g, ln):
                for r in range(NQ):
                    t, j = r // 4, r % 4
                    T = u * KT + t
                    pt = (par * KT + t) % 2
                    if k == U + 1 and r == 0:
                        pe.wait_ge(gmat_ready, 1)
                        pe.matmul(bank(0)[:, 0:3], ones[:, :], gmat[:, :], start=True, stop=True
                                  ).then_inc(gall_ready, 1)
                    if projects(k):
                        if j == 0:
                            pe.wait_ge(clo_ready, T + 1)
                            if k >= 1 or t >= 2:
                                wait(pe, khat_ready, T - 1)
                                wait(pe, vres_ready, T - 1)
                        for kc in (2 * j, 2 * j + 1):
                            if t == 0 and par == 0 and (k == 0 or not (isinstance(g, int) and g == 0)) and not ln:
                                pe.wait_ge(wklo_ready, g * KC + (kc + 1))
                            for n, (a, w) in enumerate(((chi, wkhi), (chi, wklo), (clo, wkhi))):
                                mm = pe.matmul(bank(pt)[0:KW, :], a[:, pt, kc, :], w[:, kc, :],
                                               start=(kc == 0 and n == 0), stop=(kc == KC - 1 and n == 2))
                        if j == 3:
                            mm.then_inc(kv_ready, 1)
                    if attends(k, r, SHIFT):
                        e = r - SHIFT
                        ap = 1 - par if e >= 0 else par
                        hd, c = (e % NQ) // 3, e % 3
                        R = (u - 1) * NQ + e
                        if e in (0, 1, 2):
                            pe.wait_ge(kst_ready, (u - 1) * KT + 2 * c + 2)
                        if e == 0:
                            pe.wait_ge(q_in[ap], (u - 1 - ap) * 8 + 16)
                        if not (k == 1 and e < 3):
                            pe.wait_ge(p_ready, R - 2)
                        for n in range(2):
                            kt = 2 * c + n
                            mm = pe.matmul(bank(3 + e % 3)[0:KW, S * n:S * n + S],
                                           kst[:, ap, hd, KW * kt:KW * kt + KW], qT[:, ap, hd, :],
                                           start=True, stop=True)
                        mm.then_inc(s_ready, 1)
                    if attends(k, r, SHIFT + LAG):
                        e = r - SHIFT - LAG
                        ap = 1 - par if e >= 0 else par
                        hd, c = (e % NQ) // 3, e % 3
                        R = (u - 1) * NQ + e
                        sl = e % 6
                        pair = hd // 2
                        if e == 0:
                            pe.wait_ge(v3_ready, u * KT + 1)
                        if e % 6 == 0 and not (k == 1 and e < 12):
                            pe.wait_ge(o_ready, (u - 1) * 8 + 2 * (e // 6) - 2)
                        pe.wait_ge(plo_ready, R + 1)
                        for qt, nq in enumerate(QROWS):
                            c0 = 2 * VW * qt + VW * (hd % 2)
                            o = bank(6 + pair % 2)
                            for n in range(2):
                                kt = 2 * c + n
                                q = slice(P * qt, P * qt + nq)
                                mm = pe.matmul(o[0:nq, c0:c0 + VW], phi[0:KW, sl, n, q], val[0:KW, ap, kt, hd, :],
                                               start=(e % 6 == 0 and qt == 0 and n == 0), stop=False,
                                               skip_group_check=True)
                                mm = pe.matmul(o[0:nq, c0 + DH:c0 + VW], plo[0:KW, sl, n, q],
                                               val[0:KW, ap, kt, hd, DH:VW], start=False,
                                               stop=(e % 6 == 5 and n == 1), skip_group_check=True)
                        mm.then_inc(pv_done, 1)
                    if j == 1 and behind(k, t, 2):
                        pn = pt
                        pe.wait_ge(klo_ready, T - 1)
                        wait(pe, kst_ready, T - 2)
                        for h in range(HG):
                            mm = pe.transpose(bank(2, F16)[:, h * P:h * P + KW],
                                              knat[0:KW, pn, h, :, :].rearrange("p a d -> p (a d)"),
                                              identh[0:KW, 0:KW])
                        mm.then_inc(kT_ready, 1)

            units(pe, unit_b)

            phase_b_over(pe)

            def xn_transpose(i):
                pe.wait_ge(stage_in[i % 4], 16 * (i // 4 + 1))
                wait(pe, xnTh_ready, i - 1)
                wait(pe, xnTl_ready, i - 1)
                for part in range(2):
                    for kc in range(KC):
                        mm = pe.transpose(bank(4 + 2 * (i % 2) + part, F16)[:, kc * P:kc * P + LT],
                                          stage[:, i % 4, part, kc * P:kc * P + P], identh[0:LT, 0:LT])
                mm.then_inc(cnT_ready, 1)

            for i in X_TRANSPOSED[0]:
                xn_transpose(i)

            def hidden(j, s, first):
                if first:
                    pe.wait_ge(thr_step, 3)
                pe.wait_ge(wquant_ready, j * 3 + 2)
                for c, (c0, n) in enumerate(CH):
                    if first:
                        pe.wait_ge(xnTh_ready, -(-(c0 + n) // LT))
                        pe.wait_ge(xnTl_ready, -(-(c0 + n) // LT))
                    if not (first and c < 2):
                        pe.wait_ge(hf_ready, j * 4 + c - 1)
                    for m in range(2):
                        o = bank(2 * m + c % 2)[:, 0:n]
                        for kc in range(KC):
                            for part, xt in enumerate((xnTh, xnTl)):
                                mm = pe.matmul(o, w12q[:, s, m, kc, :], xt[:, kc, c0:c0 + n],
                                               start=(kc == 0 and part == 0), stop=(kc == KC - 1 and part == 1))
                        if first and m == 0:
                            for i in X_TRANSPOSED[2 * c + 1]:
                                xn_transpose(i)
                    mm.then_inc(h_ready, 1)
                    if first and c < 3:
                        for i in X_TRANSPOSED[2 * c + 2]:
                            xn_transpose(i)

            hidden(0, 0, True)
            hidden(1, 1, False)
            with pe.Fori(1, FJ // 2) as pair:
                for s in range(2):
                    hidden(pair * 2 + s, s, False)

            pe.wait_ge(wquant_ready, 3 * FJ)
            pe.wait_ge(hf_ready, 4 * FJ)

            def result(m, par, first):
                pe.wait_ge(hid_in[par], (m - par) * 8 + 16)
                for tt in range(2):
                    if not first:
                        pe.wait_ge(ob_ready, m * 2 + tt - 3)
                    for c in range(2):
                        for j in range(FJ):
                            for part in range(2):
                                mm = pe.matmul(bank(4 * par + 2 * tt + c),
                                               hid[par][:, j, part, P * tt:P * tt + P],
                                               w3q[:, j, 512 * c:512 * c + 512],
                                               start=(j == 0 and part == 0), stop=(j == FJ - 1 and part == 1))
                    mm.then_inc(y_ready, 1)

            result(0, 0, True)
            result(1, 1, True)
            result(2, 0, False)
            with pe.Fori(1, NM // 2) as pair:
                result(pair * 2 + 1, 1, False)
                result(pair * 2 + 2, 0, False)


def kernel(x, ctx_2048, g_xattn, g_ffn, L0_xattn_Wq, L0_xattn_Wk, L0_xattn_Wv, L0_ffn_w1, L0_ffn_w2, L0_ffn_w3):
    import numpy as np
    import concourse.bacc as bacc
    from concourse.bass_utils import run_bass_kernel_spmd

    def c(a):
        return np.ascontiguousarray(a)

    wkv = np.concatenate([np.asarray(L0_xattn_Wk), np.asarray(L0_xattn_Wv)], axis=0)
    wkv = wkv.reshape(G, GC, 2, KC, P).transpose(0, 4, 3, 2, 1).reshape(G, P, KC, 512)
    w12 = [np.asarray(w).reshape(FJ, P, KC, P).transpose(0, 3, 2, 1).reshape(FJ, P, D)
           for w in (L0_ffn_w1, L0_ffn_w2)]
    w3 = np.asarray(L0_ffn_w3).T.reshape(FJ, P, D)
    wffn = np.stack([*w12, w3]).reshape(WPAIRS, 2, P, D).transpose(0, 2, 1, 3)
    arrays = {
        "in_x": c(np.asarray(x).reshape(NT, P, D)),
        "in_ctx": c(np.asarray(ctx_2048).reshape(B * KT, KW, KC, P).transpose(0, 3, 2, 1)),
        "in_wq": c(np.asarray(L0_xattn_Wq).reshape(D, KC, P).transpose(2, 1, 0)),
        "in_wkv": c(wkv),
        "in_wffn": c(wffn),
        "in_gates": c(np.broadcast_to(np.concatenate([np.asarray(g_xattn), np.asarray(g_ffn)])[None, :], (P, 2))),
    }
    nc = bacc.Bacc("TRN2", target_bir_lowering=False, num_devices=1)
    args = [nc.dram_tensor(n, a.shape, F32, kind="ExternalInput").ap() for n, a in arrays.items()]
    out = nc.dram_tensor("out", (TOK, D), F32, kind="ExternalOutput").ap()
    flamingo_kernel(nc, *args, out)
    r = run_bass_kernel_spmd(nc, [arrays], core_ids=[0])
    return r.results[0]["out"].reshape(B, S, D)
```
